# Optimizing a Trainium2 kernel written in Bass

```python
import numpy as np
import jax
import jax.numpy as jnp

def _softmax(x, axis=-1):
    return jax.nn.softmax(x, axis=axis)

def _gelu(x):
    return jax.nn.gelu(x, approximate=True)

def _silu(x):
    return jax.nn.silu(x)

def _sigmoid(x):
    return jax.nn.sigmoid(x)

def _layernorm(x, axis=-1, eps=1e-05):
    m = jnp.mean(x, axis=axis, keepdims=True)
    v = jnp.var(x, axis=axis, keepdims=True)
    return (x - m) / jnp.sqrt(v + eps)

def _scatter_add(tgt, idx, src, axis=0):
    return tgt.at[idx].add(src)

def _segment_sum(src, seg, n):
    return jax.ops.segment_sum(src, seg, n)
kernel_name = 'mk_decoder_postln_d2_seqx_r8_881eb0'

def setup_inputs(seed: int=0):
    np.random.seed(seed)
    _w = jnp.asarray

    def _rec_inputs():
        import jax
        import jax.numpy as jnp
        _rk = jax.random.key(seed)
        x = 7.22e-05 + 1 * jax.random.normal(jax.random.fold_in(_rk, 1), (4, 512, 128), jnp.float32)
        _lenS = 512 - jax.random.randint(jax.random.fold_in(_rk, 7), (4,), 0, max(1, 512 // 4) + 1, jnp.int32)
        _lenS2 = 77 - jax.random.randint(jax.random.fold_in(_rk, 8), (4,), 0, max(1, 77 // 4) + 1, jnp.int32)
        _ctx_1024P = jax.random.normal(jax.random.fold_in(_rk, 11), (4, 16, 128), jnp.float32)
        _ctx_1024c = jax.random.dirichlet(jax.random.fold_in(_rk, 511), 0.3 * jnp.ones((16,), jnp.float32), (4, 77))
        _ctx_1024t = jnp.einsum('bsk,bkd->bsd', _ctx_1024c, _ctx_1024P)
        _ctx_1024t = _ctx_1024t * jax.lax.rsqrt(jnp.mean(jnp.square(_ctx_1024t)) + 1e-12) * 0.953939
        ctx_1024 = 4.13588e-05 + 0.999923 * (_ctx_1024t + 0.3 * jax.random.normal(jax.random.fold_in(_rk, 611), (4, 77, 128), jnp.float32))
        return (x, ctx_1024)
    x, ctx_1024 = _rec_inputs()

    def _L0_attn_setup():
        import jax, jax.numpy as jnp
        import numpy as np
        D_K, D_MODEL, NUM_HEADS = (64, 128, 16)

        def _xavier(key, shape):
            fan_in, fan_out = (shape[-2], shape[-1])
            limit = float(np.sqrt(6.0 / (fan_in + fan_out)))
            return jax.random.uniform(key, shape, jnp.float32, -limit, limit)
        key = jax.random.key(seed)
        kx, kq, kk, kv, ko = jax.random.split(key, 5)
        x = jax.random.normal(kx, (2, 256, D_MODEL), dtype=jnp.float32)
        w_q = _xavier(kq, (NUM_HEADS, D_MODEL, D_K))
        w_k = _xavier(kk, (NUM_HEADS, D_MODEL, D_K))
        w_v = _xavier(kv, (NUM_HEADS, D_MODEL, D_K))
        w_o = _xavier(ko, (NUM_HEADS * D_K, D_MODEL))
        return {'x': x, 'w_q': w_q, 'w_k': w_k, 'w_v': w_v, 'w_o': w_o}
    _L0_attn_all = _L0_attn_setup()
    _L0_attn_in = {k: v for k, v in _L0_attn_all.items() if k in ('w_q', 'w_k', 'w_v', 'w_o')}
    del _L0_attn_all

    def _L0_xattn_setup():
        import jax, jax.numpy as jnp
        import numpy as np
        B, S, D, H = (4, 256, 128, 16)
        DK = D // H
        key = jax.random.key(seed)
        ks = jax.random.split(key, 8)
        scale = 1.0 / np.sqrt(D)
        return {'q': jax.random.normal(ks[0], (B, S, D), jnp.float32), 'k': jax.random.normal(ks[1], (B, S, D), jnp.float32), 'v': jax.random.normal(ks[2], (B, S, D), jnp.float32), 'wq': jax.random.normal(ks[3], (D, D), jnp.float32) * scale, 'bq': jnp.zeros((D,), jnp.float32), 'wk': jax.random.normal(ks[4], (D, D), jnp.float32) * scale, 'bk': jnp.zeros((D,), jnp.float32), 'wv': jax.random.normal(ks[5], (D, D), jnp.float32) * scale, 'bv': jnp.zeros((D,), jnp.float32), 'wo': jax.random.normal(ks[6], (D, D), jnp.float32) * scale, 'bo': jnp.zeros((D,), jnp.float32)}
    _L0_xattn_all = _L0_xattn_setup()
    _L0_xattn_in = {k: v for k, v in _L0_xattn_all.items() if k in ('wq', 'bq', 'wk', 'bk', 'wv', 'bv', 'wo', 'bo')}
    del _L0_xattn_all

    def _L0_ffn_setup():
        import jax, jax.numpy as jnp
        import numpy as np
        B, T, D = (4, 128, 128)
        E, K, F_EXP = (8, 2, 128)
        NUM_BLOCK = 12
        key = jax.random.key(seed)
        k_x, k_b, k_r, k_1, k_2 = jax.random.split(key, 5)
        x = jax.random.normal(k_x, (B, T, D), dtype=jnp.float32)
        auxfree_bias = jax.random.normal(k_b, (E,), dtype=jnp.float32) * 0.1
        router_w = jax.random.normal(k_r, (E, D), dtype=jnp.float32) * 0.02
        w1 = jax.random.normal(k_1, (E, F_EXP, D), dtype=jnp.float32) * 0.02
        w2 = jax.random.normal(k_2, (E, D, F_EXP), dtype=jnp.float32) * (0.02 / np.sqrt(2.0 * NUM_BLOCK))
        return {'x': x, 'auxfree_bias': auxfree_bias, 'router_w': router_w, 'w1': w1, 'w2': w2}
    _L0_ffn_all = _L0_ffn_setup()
    _L0_ffn_in = {k: v for k, v in _L0_ffn_all.items() if k in ('auxfree_bias', 'router_w', 'w1', 'w2')}
    del _L0_ffn_all

    def _L1_attn_setup():
        import jax, jax.numpy as jnp
        import numpy as np
        N, L, E = (4, 256, 128)
        HID, HEADS = (128, 16)
        key = jax.random.key(seed)
        ks = jax.random.split(key, 9)
        s = 1.0 / np.sqrt(E)
        return {'X_embed': jax.random.normal(ks[0], (N, L, E), dtype=jnp.float32), 'W_q': jax.random.normal(ks[1], (E, HID), dtype=jnp.float32) * s, 'b_q': jax.random.normal(ks[2], (HID,), dtype=jnp.float32) * 0.01, 'W_k': jax.random.normal(ks[3], (E, HID), dtype=jnp.float32) * s, 'b_k': jax.random.normal(ks[4], (HID,), dtype=jnp.float32) * 0.01, 'W_v': jax.random.normal(ks[5], (E, HID), dtype=jnp.float32) * s, 'b_v': jax.random.normal(ks[6], (HID,), dtype=jnp.float32) * 0.01, 'W_o': jax.random.normal(ks[7], (HID, HID), dtype=jnp.float32) * (1.0 / np.sqrt(HID)), 'b_o': jax.random.normal(ks[8], (HID,), dtype=jnp.float32) * 0.01}
    _L1_attn_all = _L1_attn_setup()
    _L1_attn_in = {k: v for k, v in _L1_attn_all.items() if k in ('W_q', 'b_q', 'W_k', 'b_k', 'W_v', 'b_v', 'W_o', 'b_o')}
    del _L1_attn_all

    def _L1_xattn_setup():
        import jax, jax.numpy as jnp
        import numpy as np
        DIM = 128
        HEADS = 16
        DIM_HEAD = 64
        INNER = HEADS * DIM_HEAD
        EPS = 1e-05

        def _layernorm(x, w, b):
            m = jnp.mean(x, axis=-1, keepdims=True)
            v = jnp.mean(jnp.square(x - m), axis=-1, keepdims=True)
            return (x - m) * jax.lax.rsqrt(v + EPS) * w + b
        key = jax.random.key(seed)
        ks = jax.random.split(key, 9)
        B, N, L = (8, 512, 64)
        x = jax.random.normal(ks[0], (B, N, DIM), dtype=jnp.float32)
        latents = jax.random.normal(ks[1], (B, L, DIM), dtype=jnp.float32)
        s = 1.0 / np.sqrt(DIM)
        Wq = jax.random.normal(ks[2], (DIM, INNER), dtype=jnp.float32) * s
        Wkv = jax.random.normal(ks[3], (DIM, 2 * INNER), dtype=jnp.float32) * s
        Wo = jax.random.normal(ks[4], (INNER, DIM), dtype=jnp.float32) * (1.0 / np.sqrt(INNER))
        ln1_w = jnp.ones((DIM,), jnp.float32)
        ln1_b = jnp.zeros((DIM,), jnp.float32)
        ln2_w = jnp.ones((DIM,), jnp.float32)
        ln2_b = jnp.zeros((DIM,), jnp.float32)
        return {'x': x, 'latents': latents, 'Wq': Wq, 'Wkv': Wkv, 'Wo': Wo, 'ln1_w': ln1_w, 'ln1_b': ln1_b, 'ln2_w': ln2_w, 'ln2_b': ln2_b}
    _L1_xattn_all = _L1_xattn_setup()
    _L1_xattn_in = {k: v for k, v in _L1_xattn_all.items() if k in ('Wq', 'Wkv', 'Wo', 'ln1_w', 'ln1_b', 'ln2_w', 'ln2_b')}
    del _L1_xattn_all

    def _L1_ffn_setup():
        import jax, jax.numpy as jnp
        import numpy as np
        B, T, C, H, E = (1, 32, 128, 256, 8)
        STD = 0.02
        key = jax.random.key(seed)
        ks = jax.random.split(key, 8)
        f32 = jnp.float32
        return {'x': jax.random.normal(ks[0], (B, T, C), f32), 'up': jax.random.normal(ks[1], (E, H, C), f32) * STD, 'gate': jax.random.normal(ks[2], (E, H, C), f32) * STD, 'down': jax.random.normal(ks[3], (E, C, H), f32) * STD, 'router': jax.random.normal(ks[4], (E, C), f32) * STD, 'w_up_s': jax.random.normal(ks[5], (H, C), f32) * STD, 'w_gate_s': jax.random.normal(ks[6], (H, C), f32) * STD, 'w_down_s': jax.random.normal(ks[7], (C, H), f32) * STD}
    _L1_ffn_all = _L1_ffn_setup()
    _L1_ffn_in = {k: v for k, v in _L1_ffn_all.items() if k in ('up', 'gate', 'down', 'router', 'w_up_s', 'w_gate_s', 'w_down_s')}
    del _L1_ffn_all
    return {'x': x, 'ctx_1024': ctx_1024, 'L0_attn_w_q': _L0_attn_in['w_q'], 'L0_attn_w_k': _L0_attn_in['w_k'], 'L0_attn_w_v': _L0_attn_in['w_v'], 'L0_attn_w_o': _L0_attn_in['w_o'], 'L0_xattn_wq': _L0_xattn_in['wq'], 'L0_xattn_bq': _L0_xattn_in['bq'], 'L0_xattn_wk': _L0_xattn_in['wk'], 'L0_xattn_bk': _L0_xattn_in['bk'], 'L0_xattn_wv': _L0_xattn_in['wv'], 'L0_xattn_bv': _L0_xattn_in['bv'], 'L0_xattn_wo': _L0_xattn_in['wo'], 'L0_xattn_bo': _L0_xattn_in['bo'], 'L0_ffn_auxfree_bias': _L0_ffn_in['auxfree_bias'], 'L0_ffn_router_w': _L0_ffn_in['router_w'], 'L0_ffn_w1': _L0_ffn_in['w1'], 'L0_ffn_w2': _L0_ffn_in['w2'], 'L1_attn_W_q': _L1_attn_in['W_q'], 'L1_attn_b_q': _L1_attn_in['b_q'], 'L1_attn_W_k': _L1_attn_in['W_k'], 'L1_attn_b_k': _L1_attn_in['b_k'], 'L1_attn_W_v': _L1_attn_in['W_v'], 'L1_attn_b_v': _L1_attn_in['b_v'], 'L1_attn_W_o': _L1_attn_in['W_o'], 'L1_attn_b_o': _L1_attn_in['b_o'], 'L1_xattn_Wq': _L1_xattn_in['Wq'], 'L1_xattn_Wkv': _L1_xattn_in['Wkv'], 'L1_xattn_Wo': _L1_xattn_in['Wo'], 'L1_xattn_ln1_w': _L1_xattn_in['ln1_w'], 'L1_xattn_ln1_b': _L1_xattn_in['ln1_b'], 'L1_xattn_ln2_w': _L1_xattn_in['ln2_w'], 'L1_xattn_ln2_b': _L1_xattn_in['ln2_b'], 'L1_ffn_up': _L1_ffn_in['up'], 'L1_ffn_gate': _L1_ffn_in['gate'], 'L1_ffn_down': _L1_ffn_in['down'], 'L1_ffn_router': _L1_ffn_in['router'], 'L1_ffn_w_up_s': _L1_ffn_in['w_up_s'], 'L1_ffn_w_gate_s': _L1_ffn_in['w_gate_s'], 'L1_ffn_w_down_s': _L1_ffn_in['w_down_s']}

def reference(x, ctx_1024, L0_attn_w_q, L0_attn_w_k, L0_attn_w_v, L0_attn_w_o, L0_xattn_wq, L0_xattn_bq, L0_xattn_wk, L0_xattn_bk, L0_xattn_wv, L0_xattn_bv, L0_xattn_wo, L0_xattn_bo, L0_ffn_auxfree_bias, L0_ffn_router_w, L0_ffn_w1, L0_ffn_w2, L1_attn_W_q, L1_attn_b_q, L1_attn_W_k, L1_attn_b_k, L1_attn_W_v, L1_attn_b_v, L1_attn_W_o, L1_attn_b_o, L1_xattn_Wq, L1_xattn_Wkv, L1_xattn_Wo, L1_xattn_ln1_w, L1_xattn_ln1_b, L1_xattn_ln2_w, L1_xattn_ln2_b, L1_ffn_up, L1_ffn_gate, L1_ffn_down, L1_ffn_router, L1_ffn_w_up_s, L1_ffn_w_gate_s, L1_ffn_w_down_s):
    import jax
    import jax.numpy as jnp

    def _L0_attn_ref(x, w_q, w_k, w_v, w_o):
        import jax, jax.numpy as jnp
        import numpy as np
        D_K, D_MODEL, NUM_HEADS = (64, 128, 16)

        def _xavier(key, shape):
            fan_in, fan_out = (shape[-2], shape[-1])
            limit = float(np.sqrt(6.0 / (fan_in + fan_out)))
            return jax.random.uniform(key, shape, jnp.float32, -limit, limit)
        scale = 1.0 / jnp.sqrt(jnp.asarray(D_K, dtype=jnp.float32))
        q = jnp.einsum('bsd,hdk->bhsk', x, w_q)
        k = jnp.einsum('bsd,hdk->bhsk', x, w_k)
        v = jnp.einsum('bsd,hdk->bhsk', x, w_v)
        scores = jnp.einsum('bhqk,bhmk->bhqm', q, k) * scale
        weights = jax.nn.softmax(scores, axis=-1)
        z = jnp.einsum('bhqm,bhmk->bhqk', weights, v)
        b, h, s, dk = z.shape
        z = jnp.transpose(z, (0, 2, 1, 3)).reshape(b, s, h * dk)
        z = jnp.einsum('bse,ed->bsd', z, w_o)
        return x + z

    def _L0_xattn_ref(q, k, v, wq, bq, wk, bk, wv, bv, wo, bo):
        import jax, jax.numpy as jnp
        import numpy as np
        B, S, D, H = (4, 256, 128, 16)
        DK = D // H
        b, s, _ = q.shape

        def proj(x, w, bias):
            y = x @ w + bias
            return y.reshape(b, -1, H, DK).transpose(0, 2, 1, 3)
        qh, kh, vh = (proj(q, wq, bq), proj(k, wk, bk), proj(v, wv, bv))
        scores = jnp.einsum('bhqd,bhkd->bhqk', qh, kh) / np.sqrt(DK).astype(jnp.float32)
        attn = jax.nn.softmax(scores, axis=-1)
        out = jnp.einsum('bhqk,bhkd->bhqd', attn, vh)
        out = out.transpose(0, 2, 1, 3).reshape(b, s, D)
        return out @ wo + bo

    def _L0_ffn_ref(x, auxfree_bias, router_w, w1, w2):
        import jax, jax.numpy as jnp
        import numpy as np
        B, T, D = (4, 128, 128)
        E, K, F_EXP = (8, 2, 128)
        NUM_BLOCK = 12
        logits = jnp.einsum('btd,ed->bte', x, router_w)
        biased = jax.lax.stop_gradient(logits) + auxfree_bias
        _, idx = jax.lax.top_k(biased, K)
        gathered = jnp.take_along_axis(logits, idx, axis=-1)
        probs = jax.nn.softmax(gathered, axis=-1)
        combine = jnp.sum(jax.nn.one_hot(idx, E, dtype=x.dtype) * probs[..., None], axis=2)
        out = jnp.zeros_like(x)
        for e in range(E):
            h = jax.nn.gelu(jnp.einsum('btd,fd->btf', x, w1[e]), approximate=False)
            out = out + combine[:, :, e:e + 1] * jnp.einsum('btf,df->btd', h, w2[e])
        return out

    def _L1_attn_ref(X_embed, W_q, b_q, W_k, b_k, W_v, b_v, W_o, b_o):
        import jax, jax.numpy as jnp
        import numpy as np
        N, L, E = (4, 256, 128)
        HID, HEADS = (128, 16)
        heads = HEADS
        n, l, _ = X_embed.shape
        hid = W_q.shape[1]
        d = hid // heads
        scale = 1.0 / np.sqrt(hid).astype(np.float32)
        Q = X_embed @ W_q + b_q
        K = X_embed @ W_k + b_k
        V = X_embed @ W_v + b_v
        Q = (Q * scale).reshape(n, heads, l, d)
        K = (K * scale).reshape(n, heads, l, d)
        V = V.reshape(n, heads, l, d)
        scores = jnp.einsum('neax,nebx->neab', Q, K)
        A = jax.nn.softmax(scores, axis=2)
        diag = jnp.diagonal(A, axis1=2, axis2=3)
        out = diag[..., None] * V
        out = out.reshape(n, l, hid)
        return out @ W_o + b_o

    def _L1_xattn_ref(x, latents, Wq, Wkv, Wo, ln1_w, ln1_b, ln2_w, ln2_b):
        import jax, jax.numpy as jnp
        import numpy as np
        DIM = 128
        HEADS = 16
        DIM_HEAD = 64
        INNER = HEADS * DIM_HEAD
        EPS = 1e-05

        def _layernorm(x, w, b):
            m = jnp.mean(x, axis=-1, keepdims=True)
            v = jnp.mean(jnp.square(x - m), axis=-1, keepdims=True)
            return (x - m) * jax.lax.rsqrt(v + EPS) * w + b
        B, L, _ = latents.shape
        xn = _layernorm(x, ln1_w, ln1_b)
        ln = _layernorm(latents, ln2_w, ln2_b)
        q = ln @ Wq
        kv_input = jnp.concatenate([xn, ln], axis=-2)
        kv = kv_input @ Wkv
        k, v = jnp.split(kv, 2, axis=-1)

        def heads(t):
            b, s, _ = t.shape
            return t.reshape(b, s, HEADS, DIM_HEAD).transpose(0, 2, 1, 3)
        q, k, v = (heads(q), heads(k), heads(v))
        scale = 1.0 / np.sqrt(np.sqrt(DIM_HEAD))
        logits = jnp.einsum('bhld,bhsd->bhls', q * scale, k * scale)
        w = jax.nn.softmax(logits.astype(jnp.float32), axis=-1).astype(logits.dtype)
        out = jnp.einsum('bhls,bhsd->bhld', w, v)
        out = out.transpose(0, 2, 1, 3).reshape(B, L, INNER)
        return out @ Wo

    def _L1_ffn_ref(x, up, gate, down, router, w_up_s, w_gate_s, w_down_s):
        import jax, jax.numpy as jnp
        import numpy as np
        B, T, C, H, E = (1, 32, 128, 256, 8)
        STD = 0.02
        b, t, c = x.shape
        x_ = x.reshape(b * t, c)
        logits = x_ @ router.T
        idx = jnp.argmax(logits, axis=-1)
        onehot = jax.nn.one_hot(idx, router.shape[0], dtype=x.dtype)
        u = jnp.einsum('bc,ehc->ebh', x_, up)
        g = jnp.einsum('bc,ehc->ebh', x_, gate)
        h = jax.nn.silu(g) * u
        ye = jnp.einsum('ebh,ech->ebc', h, down)
        y = jnp.einsum('ebc,be->bc', ye, onehot)
        ys = jax.nn.silu(x_ @ w_gate_s.T) * (x_ @ w_up_s.T) @ w_down_s.T
        return (y + ys).reshape(b, t, c)
    x = _layernorm(x + _L0_attn_ref(x, L0_attn_w_q, L0_attn_w_k, L0_attn_w_v, L0_attn_w_o), axis=-1)
    x = _layernorm(x + _L0_xattn_ref(x, ctx_1024, ctx_1024, L0_xattn_wq, L0_xattn_bq, L0_xattn_wk, L0_xattn_bk, L0_xattn_wv, L0_xattn_bv, L0_xattn_wo, L0_xattn_bo), axis=-1)
    x = _layernorm(x + _L0_ffn_ref(x, L0_ffn_auxfree_bias, L0_ffn_router_w, L0_ffn_w1, L0_ffn_w2), axis=-1)
    x = _layernorm(x + _L1_attn_ref(x, L1_attn_W_q, L1_attn_b_q, L1_attn_W_k, L1_attn_b_k, L1_attn_W_v, L1_attn_b_v, L1_attn_W_o, L1_attn_b_o), axis=-1)
    x = _layernorm(x + _L1_xattn_ref(ctx_1024, x, L1_xattn_Wq, L1_xattn_Wkv, L1_xattn_Wo, L1_xattn_ln1_w, L1_xattn_ln1_b, L1_xattn_ln2_w, L1_xattn_ln2_b), axis=-1)
    x = _layernorm(x + _L1_ffn_ref(x, L1_ffn_up, L1_ffn_gate, L1_ffn_down, L1_ffn_router, L1_ffn_w_up_s, L1_ffn_w_gate_s, L1_ffn_w_down_s), axis=-1)
    return x

_drawn_inputs = setup_inputs


def setup_inputs(seed=0):
    import zlib

    import numpy as np

    out = dict(_drawn_inputs(seed))
    spreads = {'L0_xattn_bq': (0.0, 0.286),
     'L0_xattn_bk': (0.0, 0.8),
     'L0_xattn_bv': (0.0, 0.1),
     'L0_xattn_bo': (0.0, 0.1),
     'L1_xattn_ln1_w': (1.0, 0.6),
     'L1_xattn_ln1_b': (0.0, 0.384),
     'L1_xattn_ln2_w': (1.0, 0.2),
     'L1_xattn_ln2_b': (0.0, 0.1)}
    factors = {'L0_ffn_auxfree_bias': 8.0,
     'L0_ffn_router_w': 8.0,
     'L0_ffn_w1': 8.0,
     'L0_ffn_w2': 8.0,
     'L1_attn_W_q': 8.0,
     'L1_attn_b_q': 8.0,
     'L1_attn_W_k': 8.0,
     'L1_attn_b_k': 8.0,
     'L1_attn_W_v': 8.0,
     'L1_attn_b_v': 8.0,
     'L1_attn_W_o': 8.0,
     'L1_attn_b_o': 4.754,
     'L1_ffn_up': 6.959,
     'L1_ffn_gate': 6.842,
     'L1_ffn_down': 6.805,
     'L1_ffn_router': 7.585,
     'L1_ffn_w_up_s': 6.389,
     'L1_ffn_w_gate_s': 6.65,
     'L1_ffn_w_down_s': 6.504}
    for name, (base, spread) in spreads.items():
        noise = np.random.default_rng([zlib.crc32(name.encode()), seed]).standard_normal(out[name].shape)
        drawn = base * np.exp(spread * noise) if base else spread * noise
        out[name] = jnp.asarray(drawn.astype(out[name].dtype))
    for name, factor in factors.items():
        out[name] = (out[name] * factor).astype(out[name].dtype)
    return out
```

```python
from contextlib import ExitStack

import concourse.bass as bass
from concourse import mybir

F32 = mybir.dt.float32
F32R = mybir.dt.float32r
U32 = mybir.dt.uint32
ALU = mybir.AluOpType
ACT = mybir.ActivationFunctionType
AX = mybir.AxisListType.X

P = 128
BATCH = 4
T = 512
TT = T // P
CTX = 77
HEADS = 16
DH = 64
INNER = HEADS * DH
NC = INNER // P
DB = P // HEADS
EXP = 8
HID = 256
KEYS = T + CTX
KPAD = 592
KPIECE = KPAD // 2
TILES = HEADS * TT
CPAD = CTX + 1
EPS = 1e-5
TH = T // HEADS


QK_IN = 16 * 4 * 5


def build(nc, a):
    with ExitStack() as ctx:
        def sb(name, shape, dt=F32):
            return ctx.enter_context(nc.sbuf_tensor(name, shape, dt))

        def sem(name):
            return ctx.enter_context(nc.semaphore(name))

        signals = []

        def sig(name):
            signals.append(sem(name))
            return signals[-1]

        def sigs(tag, names):
            return {n: sig(f"{n}_{tag}") for n in names.split()}

        ps = ctx.enter_context(nc.psum_tensor("ps", [P, 8, 512], F32))
        pair = [ps[:, 2 * i:2 * i + 2, :].rearrange("p b c -> p (b c)") for i in range(3)]
        OB, YB = ps[:, 6, :], ps[:, 7, :]

        ident, tok_eye, spread = sb("ident", [P, P]), sb("tok_eye", [P, TH]), sb("spread", [P, 4, P])
        head_mask, expert_no = sb("head_mask", [P, HEADS]), sb("expert_no", [P, EXP])
        neg_half = sb("neg_half", [P, TT])
        G = {n: (sb(f"g{n}_h", [P, HEADS, P], F32R), sb(f"g{n}_l", [P, HEADS, P], F32R)) for n in "AE"}
        split_w = {n: (sb(n + "_h", [P, w], F32R), sb(n + "_l", [P, w], F32R)) for n, w in
                   (("wvA", INNER), ("wvE", INNER), ("wqB", P), ("w1C", EXP * P), ("rC", EXP), ("wD", 3 * P), ("rF", EXP))}
        plain_w = {n: sb(n, s) for n, s in
                   (("woA", [P, NC, P]), ("woE", [P, NC, P]), ("wkB", [P, P]), ("wvB", [P, P]), ("woB", [P, P]),
                    ("w2C", [P, EXP, P]), ("woD", [P, P]), ("gateF", [P, EXP + 1, HID]), ("upF", [P, EXP + 1, HID]),
                    ("downF", [P, EXP + 1, 2, P]))}
        bqB, bkB, bD, lnE = sb("bqB", [P, 1]), sb("bkB", [P, 1]), sb("bD", [P, 3]), sb("lnE", [P, 4])
        rows_w = {n: sb(n, [P, w]) for n, w in (("bvB", P), ("boB", P), ("boD", P), ("biasC", EXP))}

        x_in, c_in, cz, cT = sb("x_in", [P, TT, P]), sb("c_in", [P, P]), sb("cz", [P, P]), sb("cT", [P, CTX])
        x0, x1, res = sb("x0", [P, TT, P]), sb("x1", [P, TT, P]), sb("res", [P, TT, P])
        keyh, keyl, key32 = sb("keyh", [P, KPAD], F32R), sb("keyl", [P, KPAD], F32R), sb("key32", [P, KPAD])
        xh, xl = keyh[:, 0:T], keyl[:, 0:T]
        stats, mv, veps, rstd = sb("stats", [P, TT, 6]), sb("mv", [P, TT, 2]), sb("veps", [P, TT]), sb("rstd", [P, TT])
        negm, sums, rec, diag = (sb(n, [P, TILES]) for n in ("negm", "sums", "rec", "diag"))
        lg, biased, top, idxf, oh1, oh2, tmp, comb = (sb(n, [P, TT, EXP]) for n in
                                                      ("lg", "biased", "top", "idxf", "oh1", "oh2", "tmp", "comb"))
        idx = sb("idx", [P, TT, 8], U32)
        gl, gm, gs, gr = sb("gl", [P, TT, 2]), sb("gm", [P, TT]), sb("gs", [P, TT]), sb("gr", [P, TT])

        AW, RW = 12288, 8192
        arena, arena_r = sb("arena", [P, AW]), sb("arena_r", [P, RW], F32R)

        def parts(base, *widths):
            at, out = 0, []
            for w in widths:
                out.append(base[:, at:at + w])
                at += w
            assert at <= base.shape[1], at
            return out

        raw = parts(arena, *[h.shape[1] for h, _ in split_w.values()], *[HEADS * P] * 4)
        raw_qk = [r.rearrange("p (h d) -> p h d", h=HEADS) for r in raw[len(split_w):]]
        V, Z, pr0, pr1, pr2, ptf0, ptf1 = parts(arena, 5 * INNER, TT * INNER, KEYS, KEYS, KEYS, 5 * P, 5 * P)
        V, Z = V.rearrange("p (k n) -> p k n", k=5), Z.rearrange("p (t n) -> p t n", t=TT)
        pr, ptf = [pr0, pr1, pr2], [ptf0, ptf1]
        pt = [v.rearrange("p (k q) -> p k q", k=5) for v in ptf]
        ztf = parts(arena, NC * P, NC * P)
        zt = [v.rearrange("p (c q) -> p c q", c=NC) for v in ztf]
        xT_in = arena[:, 5 * INNER:5 * INNER + T]
        y_h0, y_h1, y_l0, y_l1 = parts(arena_r, T, T, T, T)
        y_h, y_l = [y_h0, y_h1], [y_l0, y_l1]
        kb_h, kb_l, qb_h, qb_l = parts(arena_r, HEADS * CPAD, HEADS * CPAD, T, T)
        kb = [v.rearrange("p (h j) -> p h j", h=HEADS) for v in (kb_h, kb_l)]
        q32, pb0, pb1, pbt0, pbt1, k32, khB, klB, v_b, aoB, aoT = parts(
            arena, T, HEADS * CTX, HEADS * CTX, HEADS * P, HEADS * P, CTX, CTX, CTX, P, T, T)
        pb = [v.rearrange("p (h j) -> p h j", h=HEADS) for v in (pb0, pb1)]
        pbt = [v.rearrange("p (h q) -> p h q", h=HEADS) for v in (pbt0, pbt1)]
        h0, h1, silu0, silu1 = parts(arena, 2 * T, 2 * T, T, T)
        ht = [v.rearrange("p (c t) -> p c t", c=2) for v in (h0, h1)]
        silu = [silu0, silu1]
        QW = HEADS * P
        qk_parts = parts(arena_r, QW, QW, QW, QW)
        qs = [v.rearrange("p (c t) -> p c t", c=HEADS) for v in qk_parts[0:2]]
        ks = [v.rearrange("p (e c t) -> p e c t", e=4, c=HEADS) for v in qk_parts[2:4]]
        ex0, ex1, dg, qd, kd, vT, ovT, rr, *qk_hl = parts(arena, 4 * 640, 4 * 640, 4 * P, T, T, T, T, 4 * T, T, T, T, T)
        ex, dg, rr = [ex0, ex1], dg.rearrange("p (i q) -> p i q", i=4), rr.rearrange("p (i t) -> p i t", i=4)
        qk_scratch = nc.dram_tensor("qk_scratch", [4, P, T], F32, kind="Internal").ap()

        w_in, w_hi, w_lo = sem("weights_in"), sem("weights_hi"), sem("weights_lo")
        g_mm, g_hi, g_lo, const_ok = sem("g_product"), sem("g_hi"), sem("g_lo"), sem("constants_set")
        setup_ok = sem("setup_through")
        loaded, stored = sig("batch_loaded"), sig("out_stored")
        vstep = sig("vector_step")
        var_ok, rstd_ok, xn_ok = sig("variance_ready"), sig("rstd_ready"), sig("x_ready")
        xt_mm, xh_ok, xl_ok = sig("xT_product"), sig("xT_hi"), sig("xT_lo")
        key_ok = sig("keys_scaled")
        att = {n: sigs(n, "v_mm v_act v_dve y_mm y_hi y_lo score negmax prob tr ptr pv z zt_mm zt_act zt_dve proj")
               for n in "AE"}
        B_ = sigs("B", "qkv q kb v score sub prob tr pt_act pt_dve pv ao aot_mm aot proj")
        C_ = sigs("C", "route gin gexp up act down acc")
        D_ = sigs("D", "zero qkv split scratch qk0 qk1 qk2 qk3 score negmax prob mask dsum r spread ov proj")
        F_ = sigs("F", "route up silu h down acc")

        loads = [(ident[:], a["ident"]), (tok_eye[:], a["tok_eye"]), (spread[:], a["spread"]),
                 (head_mask[:], a["head_mask"]), (expert_no[:], a["expert_no"])]
        loads += [(raw_qk[i][0:DH], a[n]) for i, n in enumerate(("wqA", "wkA", "wqE", "wkE"))]
        loads += [(raw[i], a[n]) for i, n in enumerate(split_w)]
        loads += [(t[:], a[n]) for n, t in plain_w.items()]
        loads += [(bqB[:], a["bqB"]), (bkB[:], a["bkB"]), (bD[:], a["bD"]), (lnE[:], a["lnE"])]
        loads += [(t[:], a[n].partition_broadcast(P)) for n, t in rows_w.items()]
        W_ALL = 16 * len(loads)
        setup = ctx.enter_context(ExitStack())
        block = setup.enter_context(nc.Block())

        @block.sync
        def _(sp):
            for dst, src in loads:
                sp.dma_start(dst, src).then_inc(w_in, 16)

        @block.gpsimd
        def _(pool):
            nc.gpsimd.memset(neg_half[:], -0.5).then_inc(const_ok, 1)


        @block.tensor
        def _(pe):
            pe.wait_ge(w_in, W_ALL)
            for i, n in enumerate("AE"):
                for h in range(HEADS):
                    pe.matmul(ps[:, 4 * i + h // 4, P * (h % 4):P * (h % 4) + P], raw_qk[2 * i][0:DH, h], raw_qk[2 * i + 1][0:DH, h],
                              start=True, stop=True).then_inc(g_mm, 1)

        @block.scalar
        def _(act):
            act.wait_ge(w_in, W_ALL)
            for (h, _), r in zip(split_w.values(), raw):
                nc.scalar.copy(h[:], r).then_inc(w_hi, 1)
            for i, n in enumerate("AE"):
                act.wait_ge(g_mm, HEADS * (i + 1))
                nc.scalar.mul(G[n][0][:].rearrange("p (b h) d -> p b (h d)", b=4), ps[:, 4 * i:4 * i + 4, :], DH ** -0.5
                              ).then_inc(g_hi, 1)


        @block.vector
        def _(dve):
            dve.wait_ge(w_in, W_ALL)
            nc.vector.memset(key32[:, KEYS:KPAD], 0.0).then_inc(const_ok, 1)
            for i, ((h, l), r) in enumerate(zip(split_w.values(), raw)):
                dve.wait_ge(w_hi, i + 1)
                nc.vector.tensor_tensor(l[:], r, h[:].bitcast(F32), ALU.subtract).then_inc(w_lo, 1)
            for i, n in enumerate("AE"):
                dve.wait_ge(g_hi, i + 1)
                for c in range(4):
                    g = [x[:, 4 * c:4 * c + 4, :].rearrange("p h d -> p (h d)") for x in G[n]]
                    ins = nc.vector.scalar_tensor_tensor(out=g[1], in0=ps[:, 4 * i + c, :], scalar=DH ** -0.5, in1=g[0].bitcast(F32),
                                                 op0=ALU.mult, op1=ALU.subtract)
                ins.then_inc(g_lo, 1)
            dve.wait_ge(g_lo, 2)
            nc.vector.memset(ps[:, 5, 0:P], 0.0).then_inc(const_ok, 1)


        setup.close()

        b = ctx.enter_context(nc.Fori(0, BATCH))
        body = ctx.enter_context(ExitStack())
        block = body.enter_context(nc.Block(no_gpsimd_drain=True))

        @block.sync
        def _(sp):
            one = bass.ds(b, 1)
            sp.dma_start(xT_in, a["xT"][one].rearrange("o p t -> (o p) t")).then_inc(loaded, 16)
            sp.dma_start(x_in[:], a["x"][one].rearrange("o p t d -> (o p) t d")).then_inc(loaded, 16)
            sp.dma_start(c_in[0:CTX], a["ctx"][one].rearrange("o p d -> (o p) d")).then_inc(loaded, 16)
            sp.dma_start(cT[:], a["cT"][one].rearrange("o p t -> (o p) t")).then_inc(loaded, 16)
            sp.wait_ge(D_["split"], 1)
            for i in range(4):
                sp.dma_start(qk_scratch[i], qk_hl[i]).then_inc(D_["scratch"], 16)
            sp.wait_ge(D_["zero"], 1)
            sp.wait_ge(D_["scratch"], 64)
            for u in range(4):
                if u >= 2:
                    sp.wait_ge(D_["score"], 4 * (u - 1))
                for row, (iq, ik) in enumerate(((0, 2), (1, 2), (0, 3), (1, 3))):
                    at = slice(DB * row, DB * row + DB)
                    src = qk_scratch[iq, :, u * P:(u + 1) * P].rearrange("(c x) t -> x c t", x=DB)
                    sp.dma_start(qs[u % 2][at].bitcast(F32), src).then_inc(D_[f"qk{u}"], 16)
                    for e in range(4):
                        src = qk_scratch[ik, :, u * P + TH * e:u * P + TH * e + TH].rearrange("(c x) t -> x c t", x=DB)
                        sp.dma_start(ks[u % 2][at, e].bitcast(F32), src).then_inc(D_[f"qk{u}"], 16)
            sp.wait_ge(xn_ok, 8)
            sp.dma_start(a["out"][one].rearrange("o p t d -> (o p) t d"), x1[:]).then_inc(stored, 16)
            sp.wait_ge(stored, 16)

        @block.gpsimd
        def _(pool):
            def inverse_root(b, k, rows=P, n=TT):
                pool.wait_ge(var_ok, k + 1)
                nc.gpsimd.tensor_tensor(rstd[0:rows, 0:n], veps[0:rows, 0:n], neg_half[0:rows, 0:n], ALU.pow).then_inc(rstd_ok, 1)

            inverse_root(b, 0)
            inverse_root(b, 1)
            pool.wait_ge(xn_ok, 2)
            nc.gpsimd.memset(arena_r[:].bitcast(F32), 0.0).then_inc(D_["zero"], 1)
            inverse_root(b, 2)
            for e in range(HEADS):
                pool.wait_ge(D_["prob"], 4 * e + 4)
                if e >= 1:
                    pool.wait_ge(D_["dsum"], e)
                v = ex[e % 2].rearrange("p (i k) -> p i k", k=640)[:, :, 0:P]
                nc.gpsimd.tensor_tensor(dg, v, ident[:, None, :].to_broadcast([P, 4, P]), ALU.mult).then_inc(D_["mask"], 1)
            inverse_root(b, 3)
            inverse_root(b, 4)
            inverse_root(b, 5, CTX, 1)
            inverse_root(b, 6)
            inverse_root(b, 7)

        @block.tensor
        def _(pe):
            def mm(out, lhsT, rhs, start=True, stop=True):
                return pe.matmul(out, lhsT, rhs, start=start, stop=stop, skip_group_check=True)

            def mm3(out, lhsT, rhs):
                (lh, ll), (rh, rl) = lhsT, rhs
                mm(out, lh, rh, stop=False)
                mm(out, lh, rl, start=False, stop=False)
                return mm(out, ll, rh, start=False)

            def cols(pieces, at):
                return [p[:, at] for p in pieces]

            XT = (xh, xl)
            tok = [slice(P * t, P * t + P) for t in range(TT)]

            def transpose_x(b, k, src, j):
                pe.wait_ge(xn_ok, k + 1)
                for t in range(TT):
                    ins = pe.transpose(YB[:, tok[t]], src[:, t], ident[:])
                ins.then_inc(xt_mm, 1)

            def attention(b, s, n, wv, nk, wo, kx):
                pe.wait_ge(xl_ok, kx)
                wv = split_w[wv]
                key = [slice(P * k, P * k + P) for k in range(TT)] + [slice(T, KEYS)]
                rows = [P] * TT + [CTX]
                for g in range(2 * nk):
                    k, half = divmod(g, 2)
                    if g >= 4:
                        pe.wait_ge(s["v_act"] if g % 2 == 0 else s["v_dve"], (g - 4) // 2 + 1)
                    mm3(ps[0:rows[k], g % 4, :], cols((keyh, keyl), key[k]),
                                     cols(wv, slice(512 * half, 512 * half + 512))).then_inc(s["v_mm"], 1)

                def mix_head(h):
                    if h >= 1:
                        pe.wait_ge(s["y_lo"], h)
                    mm3(YB, [g[:, h, :] for g in G[n]], XT).then_inc(s["y_mm"], 1)

                mix_head(0)
                pe.wait_ge(s["v_act"], nk)
                pe.wait_ge(s["v_dve"], nk)
                for i in range(TILES + 3):
                    if i < TILES:
                        h, q = divmod(i, TT)
                        if q == 0:
                            pe.wait_ge(s["y_lo"], h + 1)
                        if i >= 2:
                            pe.wait_ge(s["prob"], i - 1)
                        lhsT = (y_h[h % 2][:, tok[q]], y_l[h % 2][:, tok[q]])
                        if nk == TT:
                            ins = mm3(pair[i % 2][:, 0:T], lhsT, XT)
                        else:
                            for w in range(2):
                                at = 512 - KPIECE + w * KPIECE
                                ins = mm3(pair[i % 2][:, at:at + KPIECE], lhsT,
                                          cols((keyh, keyl), slice(w * KPIECE, w * KPIECE + KPIECE)))
                        ins.then_inc(s["score"], 1)
                        if q == 1 and h + 1 < HEADS:
                            mix_head(h + 1)
                    if 2 <= i < TILES + 2:
                        j = i - 2
                        pe.wait_ge(s["prob"], j + 1)
                        if j >= 1:
                            pe.wait_ge(s["ptr"], j)
                        for k in range(nk):
                            ins = pe.transpose(pair[2][0:rows[k], P * k:P * k + P], pr[j % 3][:, key[k]], ident[:])
                        ins.then_inc(s["tr"], 1)
                    if i >= 3:
                        h, q = divmod(i - 3, TT)
                        pe.wait_ge(s["ptr"], i - 2)
                        if q == 0 and h >= 1:
                            pe.wait_ge(s["z"], h)
                        for k in range(nk):
                            ins = mm(OB[:, DH * q:DH * q + DH], pt[(i - 3) % 2][0:rows[k], k, :],
                                     V[0:rows[k], k, DH * h:DH * h + DH], start=k == 0, stop=k == nk - 1)
                        ins.then_inc(s["pv"], 1)
                pe.wait_ge(s["z"], HEADS)
                for q in range(TT + 1):
                    if q < TT:
                        if q >= 2:
                            pe.wait_ge(s["zt_act"] if q % 2 == 0 else s["zt_dve"], 1)
                        for c in range(NC):
                            ins = pe.transpose(pair[q % 2][:, P * c:P * c + P], Z[:, q, P * c:P * c + P], ident[:])
                        ins.then_inc(s["zt_mm"], 1)
                    if q >= 1:
                        pe.wait_ge(s["zt_act"] if (q - 1) % 2 == 0 else s["zt_dve"], (q - 1) // 2 + 1)
                        for c in range(NC):
                            ins = mm(YB[:, tok[q - 1]], zt[(q - 1) % 2][:, c, :], plain_w[wo][:, c, :],
                                     start=c == 0, stop=c == NC - 1)
                ins.then_inc(s["proj"], 1)

            def project(b, s, ready, srcT, w, out):
                pe.wait_ge(ready, 1)
                for t in range(TT):
                    ins = mm(out[:, tok[t]], srcT[:, tok[t]], w[:])
                ins.then_inc(s["proj"], 1)

            def small_heads(b):
                s = B_
                pe.wait_ge(xl_ok, 2)
                mm3(ps[:, 0, :], cols(split_w["wqB"], slice(0, P)), XT).then_inc(s["qkv"], 1)
                mm(ps[:, 1, 0:CTX], plain_w["wkB"][:], cT[:]).then_inc(s["qkv"], 1)
                mm(ps[0:CTX, 2, 0:P], cT[:], plain_w["wvB"][:]).then_inc(s["qkv"], 1)
                pe.wait_ge(s["q"], 1)
                pe.wait_ge(s["kb"], 1)
                pe.wait_ge(s["v"], 1)
                for i in range(TT + 1):
                    if i < TT:
                        if i >= 1:
                            pe.wait_ge(s["sub"], i)
                        for g in range(4):
                            at = slice(4 * CPAD * g, 4 * CPAD * (g + 1))
                            ins = mm3(ps[:, g, 0:4 * CPAD], (qb_h[:, tok[i]], qb_l[:, tok[i]]), (kb_h[:, at], kb_l[:, at]))
                        ins.then_inc(s["score"], 1)
                    if i >= 1:
                        q = i - 1
                        pe.wait_ge(s["prob"], q + 1)
                        for g in range(4):
                            n = 4 * q + g
                            if n >= 2:
                                pe.wait_ge(s["pt_act"] if n % 2 == 0 else s["pt_dve"], (n - 2) // 2 + 1)
                            for h in range(4 * g, 4 * g + 4):
                                ins = pe.transpose(ps[0:CTX, 4 + g % 2, P * (h % 4):P * (h % 4) + P], pb[q % 2][:, h, :],
                                                   ident[:])
                            ins.then_inc(s["tr"], 1)
                        pe.wait_ge(s["pt_act"], 2 * q + 2)
                        pe.wait_ge(s["pt_dve"], 2 * q + 2)
                        if q >= 1:
                            pe.wait_ge(s["ao"], q)
                        for h in range(HEADS):
                            ins = mm(OB[:, DB * h:DB * h + DB], pbt[q % 2][0:CTX, h, :], v_b[0:CTX, DB * h:DB * h + DB])
                        ins.then_inc(s["pv"], 1)
                pe.wait_ge(s["ao"], TT)
                for t in range(TT):
                    ins = pe.transpose(YB[:, tok[t]], aoB[:, tok[t]], ident[:])
                ins.then_inc(s["aot_mm"], 1)
                project(b, s, s["aot"], aoT, plain_w["woB"], OB)

            def route(b, s, w, kx):
                pe.wait_ge(xl_ok, kx)
                for t in range(TT):
                    ins = mm3(YB[:, EXP * t:EXP * t + EXP], (xh[:, tok[t]], xl[:, tok[t]]), cols(split_w[w], slice(0, EXP)))
                ins.then_inc(s["route"], 1)

            def gelu_experts(b):
                s = C_
                route(b, s, "rC", 3)
                for e in range(EXP + 1):
                    if e < EXP:
                        if e >= 2:
                            pe.wait_ge(s["act"], e - 1)
                        mm3(ps[:, e % 2, :], cols(split_w["w1C"], slice(P * e, P * e + P)), XT).then_inc(s["up"], 1)
                    if e >= 1:
                        d = e - 1
                        pe.wait_ge(s["act"], e)
                        if d >= 2:
                            pe.wait_ge(s["acc"], d - 1)
                        for t in range(TT):
                            ins = mm(ps[:, 2 + d % 2, tok[t]], ht[d % 2][:, 0, tok[t]], plain_w["w2C"][:, d, :])
                        ins.then_inc(s["down"], 1)

            def diagonal_attention(b):
                s = D_
                pe.wait_ge(xl_ok, 4)
                for i in range(3):
                    mm3(ps[:, i, :], cols(split_w["wD"], slice(P * i, P * i + P)), XT).then_inc(s["qkv"], 1)
                for e in range(HEADS):
                    u = e // 4
                    if e % 4 == 0:
                        pe.wait_ge(s[f"qk{u}"], QK_IN)
                    if e >= 2:
                        pe.wait_ge(s["prob"], 4 * (e - 1))
                    for i in range(4):
                        ins = mm(ps[:, 4 * (e % 2) + i, :], ks[u % 2][:, e % 4, 4 * i:4 * i + 4, :].rearrange("p c t -> p (c t)"),
                                 qs[u % 2][:, :, TH * (e % 4):TH * (e % 4) + TH])
                    ins.then_inc(s["score"], 1)
                pe.wait_ge(s["r"], 1)
                for i in range(4):
                    ins = mm(ps[:, 0, :], spread[:, i, :], rr[:, i, :], start=i == 0, stop=i == 3)
                ins.then_inc(s["spread"], 1)
                project(b, s, s["ov"], ovT, plain_w["woD"], ps[:, 1, :])

            def swiglu_experts(b):
                s = F_
                route(b, s, "rF", 6)
                for j in range(2 * EXP + 4):
                    if j < 2 * EXP + 2:
                        e, c = divmod(j, 2)
                        if j >= 2:
                            pe.wait_ge(s["h"], j - 1)
                        mm(ps[:, 2 * (j % 2), :], plain_w["gateF"][:, e, P * c:P * c + P], key32[:, 0:T])
                        mm(ps[:, 2 * (j % 2) + 1, :], plain_w["upF"][:, e, P * c:P * c + P], key32[:, 0:T]).then_inc(s["up"], 1)
                    if j >= 3 and j % 2 == 1:
                        d = (j - 3) // 2
                        pe.wait_ge(s["h"], 2 * d + 2)
                        if d >= 2:
                            pe.wait_ge(s["acc"], d - 1)
                        for t in range(TT):
                            for c in range(2):
                                ins = mm(ps[:, 4 + d % 2, tok[t]], ht[d % 2][:, c, tok[t]], plain_w["downF"][:, d, c, :],
                                         start=c == 0, stop=c == 1)
                        ins.then_inc(s["down"], 1)

            attention(b, att["A"], "A", "wvA", TT, "woA", 1)
            transpose_x(b, 0, x0, 0)
            small_heads(b)
            transpose_x(b, 1, x1, 1)
            gelu_experts(b)
            transpose_x(b, 2, x0, 2)
            diagonal_attention(b)
            transpose_x(b, 4, x0, 3)
            pe.wait_ge(xn_ok, 6)
            pe.transpose(OB[:, 0:CTX], cz[0:CTX, :], ident[0:CTX, 0:CTX]).then_inc(xt_mm, 1)
            attention(b, att["E"], "E", "wvE", TT + 1, "woE", 5)
            transpose_x(b, 6, x0, 5)
            swiglu_experts(b)

        @block.scalar
        def _(act):
            def x_hi(b, j, src=None):
                if src is None:
                    act.wait_ge(xt_mm, j)
                    nc.scalar.copy(xh, YB).then_inc(xh_ok, 1)
                else:
                    nc.scalar.copy(keyh[:, 0:src.shape[1]], src).then_inc(xh_ok, 1)

            def attention(b, s, nk):
                rows = [P] * TT + [CTX]
                width = T if nk == TT else KEYS
                at = 0 if nk == TT else 512 - KPIECE
                for g in range(0, 2 * nk, 2):
                    k = g // 2
                    act.wait_ge(s["v_mm"], g + 1)
                    nc.scalar.copy(V[0:rows[k], k, 0:512], ps[0:rows[k], g % 4, :]).then_inc(s["v_act"], 1)

                def mix_hi(h):
                    act.wait_ge(s["y_mm"], h + 1)
                    if h >= 2:
                        act.wait_ge(s["score"], 4 * h - 4)
                    nc.scalar.copy(y_h[h % 2], YB).then_inc(s["y_hi"], 1)

                mix_hi(0)
                for i in range(TILES):
                    act.wait_ge(s["negmax"], i + 1)
                    if i >= 3:
                        act.wait_ge(s["tr"], i - 2)
                    nc.scalar.activation(pr[i % 3][:, 0:width], pair[i % 2][:, at:at + width], ACT.Exp,
                                                      bias=negm[:, i:i + 1], accum_out=sums[:, i:i + 1]).then_inc(s["prob"], 1)
                    if i % TT == 1 and i // TT + 1 < HEADS:
                        mix_hi(i // TT + 1)
                for q in (0, 2):
                    act.wait_ge(s["zt_mm"], q + 1)
                    nc.scalar.copy(ztf[0], pair[0]).then_inc(s["zt_act"], 1)

            act.wait_ge(loaded, 64)
            x_hi(b, 0, xT_in)
            attention(b, att["A"], TT)
            x_hi(b, 1)
            s = B_
            for q in range(TT):
                act.wait_ge(s["sub"], q + 1)
                nc.scalar.activation(pb[q % 2], pb[q % 2], ACT.Exp).then_inc(s["prob"], 1)
                for g in (0, 2):
                    act.wait_ge(s["tr"], 4 * q + g + 1)
                    nc.scalar.copy(pbt[q % 2][0:CTX, 4 * g:4 * g + 4, :].rearrange("p h q -> p (h q)"),
                                                  ps[0:CTX, 4, :]).then_inc(s["pt_act"], 1)
            act.wait_ge(s["aot_mm"], 1)
            nc.scalar.copy(aoT, YB).then_inc(s["aot"], 1)
            x_hi(b, 2)
            s = C_
            act.wait_ge(s["gin"], 1)
            nc.scalar.activation(gl[:], gl[:], ACT.Exp).then_inc(s["gexp"], 1)
            for e in range(EXP):
                act.wait_ge(s["up"], e + 1)
                if e >= 2:
                    act.wait_ge(s["down"], e - 1)
                nc.scalar.activation(ht[e % 2][:, 0, :], ps[:, e % 2, :], ACT.Gelu).then_inc(s["act"], 1)
            x_hi(b, 3)
            s = D_
            for e in range(HEADS):
                act.wait_ge(s["negmax"], e + 1)
                if e >= 2:
                    act.wait_ge(s["mask"], e - 1)
                for i in range(4):
                    c = 4 * e + i
                    nc.scalar.activation(ex[e % 2][:, T * i:T * i + T], ps[:, 4 * (e % 2) + i, :], ACT.Exp,
                                                      bias=negm[:, c:c + 1], accum_out=sums[:, c:c + 1]).then_inc(s["prob"], 1)
            act.wait_ge(key_ok, 1)
            x_hi(b, 4, key32[:])
            attention(b, att["E"], TT + 1)
            x_hi(b, 6)
            s = F_
            for j in range(2 * EXP + 2):
                act.wait_ge(s["up"], j + 1)
                if j >= 2:
                    act.wait_ge(s["h"], j - 1)
                nc.scalar.activation(silu[j % 2], ps[:, 2 * (j % 2), :], ACT.Silu).then_inc(s["silu"], 1)

        @block.vector
        def _(dve):
            v = nc.vector
            steps = [0]

            def link(ins):
                steps[0] += 1
                ins.then_inc(vstep, 1)
                dve.wait_ge(vstep, steps[0])

            def over(t, shape, axis):
                at = [slice(None)] * t.ndim
                at.insert(axis, None)
                return t[tuple(at)].to_broadcast(shape)

            def norm(b, k, src, dst, rows=P, n=TT):
                for t in range(n):
                    ins = v.bn_stats(stats[0:rows, t, :], src[0:rows, t, :])
                link(ins)
                for t in range(n):
                    ins = v.bn_aggr(mv[0:rows, t, :], stats[0:rows, t, :])
                link(ins)
                v.tensor_scalar(veps[0:rows, 0:n], mv[0:rows, 0:n, 1], EPS, None, ALU.add).then_inc(var_ok, 1)
                dve.wait_ge(rstd_ok, k + 1)
                for t in range(n):
                    ins = v.tensor_scalar(dst[0:rows, t, :], src[0:rows, t, :], mv[0:rows, t, 0:1], rstd[0:rows, t:t + 1],
                                          ALU.subtract, ALU.mult)
                return ins.then_inc(xn_ok, 1)

            def x_lo(b, j, src=None, width=T, keep=False):
                dve.wait_ge(xh_ok, j)
                if keep:
                    v.tensor_copy(key32[:, 0:T], YB)
                v.tensor_tensor(keyl[:, 0:width], YB if src is None else src, keyh[:, 0:width].bitcast(F32),
                                         ALU.subtract).then_inc(xl_ok, 1)

            def attention(b, s, nk):
                rows = [P] * TT + [CTX]
                width = T if nk == TT else KEYS
                at = 0 if nk == TT else 512 - KPIECE
                for g in range(1, 2 * nk, 2):
                    k = g // 2
                    dve.wait_ge(s["v_mm"], g + 1)
                    v.tensor_copy(V[0:rows[k], k, 512:1024], ps[0:rows[k], g % 4, :]).then_inc(s["v_dve"], 1)

                def mix_lo(h):
                    dve.wait_ge(s["y_hi"], h + 1)
                    v.tensor_tensor(y_l[h % 2], YB, y_h[h % 2].bitcast(F32), ALU.subtract).then_inc(s["y_lo"], 1)

                mix_lo(0)
                for i in range(TILES + 3):
                    if i < TILES:
                        dve.wait_ge(s["score"], i + 1)
                        v.tensor_reduce(negm[:, i:i + 1], pair[i % 2][:, at:at + width], AX, ALU.max,
                                                       negate=True).then_inc(s["negmax"], 1)
                        if i % TT == 1 and i // TT + 1 < HEADS:
                            mix_lo(i // TT + 1)
                    if 2 <= i < TILES + 2:
                        dve.wait_ge(s["tr"], i - 1)
                        if i >= 4:
                            dve.wait_ge(s["pv"], i - 3)
                        v.tensor_copy(ptf[i % 2][:, 0:P * nk], pair[2][:, 0:P * nk]).then_inc(s["ptr"], 1)
                    if i >= 3 and (i - 3) % TT == TT - 1:
                        h = (i - 3) // TT
                        c = slice(TT * h, TT * h + TT)
                        link(v.reciprocal(rec[:, c], sums[:, c]))
                        dve.wait_ge(s["pv"], i - 2)
                        v.tensor_tensor(Z[:, :, DH * h:DH * h + DH],
                                                  OB[:, 0:TT * DH].rearrange("p (t d) -> p t d", t=TT),
                                                  over(rec[:, c], [P, TT, DH], 2), ALU.mult).then_inc(s["z"], 1)
                for q in (1, 3):
                    dve.wait_ge(s["zt_mm"], q + 1)
                    v.tensor_copy(ztf[1], pair[1]).then_inc(s["zt_dve"], 1)
                dve.wait_ge(s["proj"], 1)

            tiles = lambda t: t.rearrange("p (t d) -> p t d", t=TT)

            def small_heads(b):
                s = B_
                dve.wait_ge(s["qkv"], 1)
                link(v.tensor_scalar(q32, ps[:, 0, :], bqB[:, 0:1], DB ** -0.5, ALU.add, ALU.mult))
                link(v.tensor_copy(qb_h, q32))
                v.tensor_tensor(qb_l, q32, qb_h.bitcast(F32), ALU.subtract).then_inc(s["q"], 1)
                dve.wait_ge(s["qkv"], 2)
                for x in kb:
                    v.memset(x.bitcast(F32)[:, :, CTX:CPAD], 0.0)
                link(v.tensor_scalar(k32, ps[:, 1, 0:CTX], bkB[:, 0:1], None, ALU.add))
                link(v.tensor_copy(khB.bitcast(F32R), k32))
                link(v.tensor_tensor(klB.bitcast(F32R), k32, khB, ALU.subtract))
                for x, src in zip(kb, (khB, klB)):
                    ins = v.tensor_tensor(x[:, :, 0:CTX], over(src, [P, HEADS, CTX], 1),
                                          over(head_mask[:], [P, HEADS, CTX], 2), ALU.mult)
                ins.then_inc(s["kb"], 1)
                dve.wait_ge(s["qkv"], 3)
                v.tensor_tensor(v_b[0:CTX], ps[0:CTX, 2, 0:P], rows_w["bvB"][0:CTX], ALU.add).then_inc(s["v"], 1)
                S = ps[:, 0:4, 0:4 * CPAD].rearrange("p b (h j) -> p b h j", h=4)[:, :, :, 0:CTX]
                for i in range(TT + 1):
                    if i < TT:
                        m = negm[:, HEADS * i:HEADS * i + HEADS].rearrange("p (b h) -> p b h", b=4)
                        dve.wait_ge(s["score"], i + 1)
                        link(v.tensor_reduce(m, S, AX, ALU.max))
                        v.tensor_tensor(pb[i % 2].rearrange("p (b h) j -> p b h j", b=4), S,
                                                    over(m, [P, 4, 4, CTX], 3), ALU.subtract).then_inc(s["sub"], 1)
                    if i >= 1:
                        q = i - 1
                        c = slice(HEADS * q, HEADS * q + HEADS)
                        dve.wait_ge(s["prob"], q + 1)
                        link(v.tensor_reduce(sums[:, c], pb[q % 2], AX, ALU.add))
                        link(v.reciprocal(rec[:, c], sums[:, c]))
                        for g in (1, 3):
                            dve.wait_ge(s["tr"], 4 * q + g + 1)
                            v.tensor_copy(pbt[q % 2][0:CTX, 4 * g:4 * g + 4, :].rearrange("p h q -> p (h q)"),
                                                         ps[0:CTX, 5, :]).then_inc(s["pt_dve"], 1)
                        dve.wait_ge(s["pv"], q + 1)
                        v.tensor_tensor(aoB[:, P * q:P * q + P].rearrange("p (h d) -> p h d", h=HEADS),
                                                   OB[:, 0:P].rearrange("p (h d) -> p h d", h=HEADS),
                                                   over(rec[:, c], [P, HEADS, DB], 2), ALU.mult).then_inc(s["ao"], 1)
                dve.wait_ge(s["proj"], 1)

            def pick(b, scores):
                for t in range(TT):
                    ins = v.max(top[:, t, :], scores[:, t, :])
                link(ins)
                for t in range(TT):
                    ins = v.max_index(idx[:, t, :], top[:, t, :], scores[:, t, :])
                link(ins)
                link(v.tensor_copy(idxf[:], idx[:]))

            def one_hot(dst, n):
                return v.tensor_tensor(dst[:], over(expert_no[:], [P, TT, EXP], 1),
                                       idxf[:, :, n:n + 1].to_broadcast([P, TT, EXP]), ALU.is_equal)

            def accumulate(b, s, e, x, bank, weighted=True):
                dve.wait_ge(s["down"], e + 1)
                if e >= 1:
                    dve.wait_ge(s["acc"], e)
                for t in range(TT):
                    base = (x if e == 0 else res)[:, t, :]
                    o = ps[:, bank, P * t:P * t + P]
                    if weighted:
                        ins = v.scalar_tensor_tensor(out=res[:, t, :], in0=o, scalar=comb[:, t, e:e + 1], in1=base,
                                                     op0=ALU.mult, op1=ALU.add)
                    else:
                        ins = v.tensor_tensor(res[:, t, :], o, base, ALU.add)
                ins.then_inc(s["acc"], 1)

            def gelu_experts(b):
                s = C_
                dve.wait_ge(s["route"], 1)
                logits = YB[:, 0:TT * EXP].rearrange("p (t e) -> p t e", t=TT)
                v.tensor_copy(lg[:], logits)
                link(v.tensor_tensor(biased[:], logits, over(rows_w["biasC"][:], [P, TT, EXP], 1), ALU.add))
                pick(b, biased)
                one_hot(oh1, 0)
                link(one_hot(oh2, 1))
                for n, oh in enumerate((oh1, oh2)):
                    link(v.tensor_tensor(tmp[:], lg[:], oh[:], ALU.mult))
                    link(v.tensor_reduce(gl[:, :, n:n + 1], tmp[:], AX, ALU.add))
                link(v.tensor_reduce(gm[:], gl[:], AX, ALU.max))
                v.tensor_tensor(gl[:], gl[:], over(gm[:], [P, TT, 2], 2), ALU.subtract).then_inc(s["gin"], 1)
                dve.wait_ge(s["gexp"], 1)
                link(v.tensor_reduce(gs[:], gl[:], AX, ALU.add))
                link(v.reciprocal(gr[:], gs[:]))
                link(v.tensor_tensor(gl[:], gl[:], over(gr[:], [P, TT, 2], 2), ALU.mult))
                v.tensor_tensor(comb[:], oh1[:], gl[:, :, 0:1].to_broadcast([P, TT, EXP]), ALU.mult)
                link(v.tensor_tensor(tmp[:], oh2[:], gl[:, :, 1:2].to_broadcast([P, TT, EXP]), ALU.mult))
                link(v.tensor_tensor(comb[:], comb[:], tmp[:], ALU.add))
                for e in range(EXP):
                    accumulate(b, s, e, x1, 2 + e % 2)
                dve.wait_ge(s["acc"], EXP)

            def diagonal_attention(b):
                s = D_
                for i, (dst, scale) in enumerate(((qd, P ** -0.5), (kd, P ** -0.5), (vT, None))):
                    dve.wait_ge(s["qkv"], i + 1)
                    link(v.tensor_scalar(dst, ps[:, i, :], bD[:, i:i + 1], *((scale, ALU.add, ALU.mult) if scale else
                                                                               (None, ALU.add))))
                for i, src in enumerate((qd, kd)):
                    link(v.tensor_copy(qk_hl[2 * i].bitcast(F32R), src))
                    ins = v.tensor_tensor(qk_hl[2 * i + 1].bitcast(F32R), src, qk_hl[2 * i], ALU.subtract)
                ins.then_inc(s["split"], 1)
                for e in range(HEADS + 1):
                    if e < HEADS:
                        dve.wait_ge(s["score"], e + 1)
                        v.tensor_reduce(negm[:, 4 * e:4 * e + 4], ps[:, 4 * (e % 2):4 * (e % 2) + 4, :], AX,
                                                       ALU.max, negate=True).then_inc(s["negmax"], 1)
                    if e >= 1:
                        dve.wait_ge(s["mask"], e)
                        v.tensor_reduce(diag[:, 4 * e - 4:4 * e], dg, AX, ALU.add).then_inc(s["dsum"], 1)
                link(v.reciprocal(rec[:], sums[:]))
                link(v.tensor_tensor(diag[:], diag[:], rec[:], ALU.mult))
                by_chunk = diag[:].rearrange("p (e i) -> p i e", i=4)
                for i in range(4):
                    ins = v.tensor_tensor(rr[:, i, :].rearrange("p (e t) -> p e t", e=HEADS),
                                          over(by_chunk[:, i, :], [P, HEADS, TH], 2), over(tok_eye[:], [P, HEADS, TH], 1),
                                          ALU.mult)
                ins.then_inc(s["r"], 1)
                dve.wait_ge(s["spread"], 1)
                v.tensor_tensor(ovT, ps[:, 0, :], vT, ALU.mult).then_inc(s["ov"], 1)
                dve.wait_ge(s["proj"], 1)

            def swiglu_experts(b):
                s = F_
                dve.wait_ge(s["route"], 1)
                link(v.tensor_copy(lg[:], YB[:, 0:TT * EXP].rearrange("p (t e) -> p t e", t=TT)))
                pick(b, lg)
                link(one_hot(comb, 0))
                for j in range(2 * EXP + 2):
                    e, c = divmod(j, 2)
                    dve.wait_ge(s["silu"], j + 1)
                    if e >= 2 and c == 0:
                        dve.wait_ge(s["down"], e - 1)
                    v.tensor_tensor(ht[e % 2][:, c, :], ps[:, 2 * (j % 2) + 1, :], silu[j % 2], ALU.mult).then_inc(s["h"], 1)
                    if c == 1 and e >= 1:
                        accumulate(b, s, e - 1, x0, 4 + (e - 1) % 2)
                accumulate(b, s, EXP, x0, 4 + EXP % 2, weighted=False)
                dve.wait_ge(s["acc"], EXP + 1)

            dve.wait_ge(loaded, 64)
            x_lo(b, 1, xT_in)
            attention(b, att["A"], TT)
            link(v.tensor_tensor(res[:], x_in[:], tiles(YB), ALU.add))
            link(v.tensor_tensor(res[:], res[:], x_in[:], ALU.add))
            norm(b, 0, res, x0)
            x_lo(b, 2)
            small_heads(b)
            link(v.tensor_tensor(res[:], tiles(OB), over(rows_w["boB"][:], [P, TT, P], 1), ALU.add))
            link(v.tensor_tensor(res[:], res[:], x0[:], ALU.add))
            norm(b, 1, res, x1)
            x_lo(b, 3)
            gelu_experts(b)
            norm(b, 2, res, x0)
            x_lo(b, 4)
            diagonal_attention(b)
            link(v.tensor_tensor(res[:], tiles(ps[:, 1, :]), over(rows_w["boD"][:], [P, TT, P], 1), ALU.add))
            link(v.tensor_tensor(res[:], res[:], x0[:], ALU.add))
            norm(b, 3, res, x1)
            dve.wait_ge(xn_ok, 4)
            norm(b, 4, x1, x0)
            dve.wait_ge(xn_ok, 5)
            norm(b, 5, c_in[:].rearrange("p (o d) -> p o d", o=1), cz[:].rearrange("p (o d) -> p o d", o=1), CTX, 1)
            dve.wait_ge(xt_mm, 4)
            v.tensor_scalar(key32[:, 0:T], YB, lnE[:, 2:3], lnE[:, 3:4], ALU.mult, ALU.add)
            dve.wait_ge(xt_mm, 5)
            v.tensor_scalar(key32[:, T:KEYS], OB[:, 0:CTX], lnE[:, 0:1], lnE[:, 1:2], ALU.mult, ALU.add).then_inc(key_ok, 1)
            x_lo(b, 5, key32[:], KPAD)
            attention(b, att["E"], TT + 1)
            link(v.tensor_tensor(res[:], tiles(YB), x1[:], ALU.add))
            norm(b, 6, res, x0)
            x_lo(b, 6, keep=True)
            swiglu_experts(b)
            norm(b, 7, res, x1)

        body.close()
        numbers = [s.num for s in signals]
        assert numbers == list(range(numbers[0], numbers[0] + len(numbers)))
        nc.sync.sem_clear(range(numbers[0], numbers[-1] + 1))
        nc.all_engine_barrier()


def kernel(**inputs):
    import numpy as np
    import concourse.bacc as bacc
    from concourse.bass_utils import run_bass_kernel_spmd

    x = {k: np.ascontiguousarray(v) for k, v in inputs.items()}
    f32 = np.float32
    cat = np.concatenate

    def by_head(w):
        return w.transpose(2, 1, 0)

    def out_proj(w):
        return w.reshape(NC, P, P).transpose(1, 0, 2)

    wkv = x["L1_xattn_Wkv"]
    part, col = np.arange(P), np.arange(P)
    spread = np.zeros((P, 4, P), f32)
    for i in range(4):
        spread[:, i, :] = col[None, :] // DB == 4 * i + part[:, None] // TH
    arrays = {
        "xT": x["x"].transpose(0, 2, 1), "x": x["x"].reshape(BATCH, TT, P, P).transpose(0, 2, 1, 3),
        "ctx": x["ctx_1024"], "cT": x["ctx_1024"].transpose(0, 2, 1),
        "ident": np.eye(P, dtype=f32), "spread": spread,
        "tok_eye": (part[:, None] % TH == np.arange(TH)[None, :]).astype(f32),
        "head_mask": (part[:, None] // DB == np.arange(HEADS)[None, :]).astype(f32),
        "expert_no": np.tile(np.arange(EXP, dtype=f32), (P, 1)),
        "wqA": by_head(x["L0_attn_w_q"].transpose(1, 0, 2)), "wkA": by_head(x["L0_attn_w_k"].transpose(1, 0, 2)),
        "wqE": by_head(x["L1_xattn_Wq"].reshape(P, HEADS, DH)), "wkE": by_head(wkv[:, :INNER].reshape(P, HEADS, DH)),
        "wvA": x["L0_attn_w_v"].transpose(1, 0, 2).reshape(P, INNER), "wvE": wkv[:, INNER:],
        "woA": out_proj(x["L0_attn_w_o"]), "woE": out_proj(x["L1_xattn_Wo"]),
        "wqB": x["L0_xattn_wq"], "wkB": x["L0_xattn_wk"], "wvB": x["L0_xattn_wv"], "woB": x["L0_xattn_wo"],
        "bqB": x["L0_xattn_bq"].reshape(P, 1), "bkB": x["L0_xattn_bk"].reshape(P, 1),
        "bvB": x["L0_xattn_bv"], "boB": x["L0_xattn_bo"], "boD": x["L1_attn_b_o"], "biasC": x["L0_ffn_auxfree_bias"],
        "w1C": x["L0_ffn_w1"].transpose(2, 0, 1).reshape(P, EXP * P), "w2C": x["L0_ffn_w2"].transpose(2, 0, 1),
        "rC": x["L0_ffn_router_w"].T, "rF": x["L1_ffn_router"].T,
        "wD": cat([x["L1_attn_W_q"], x["L1_attn_W_k"], x["L1_attn_W_v"]], axis=1), "woD": x["L1_attn_W_o"],
        "bD": np.stack([x["L1_attn_b_q"], x["L1_attn_b_k"], x["L1_attn_b_v"]], axis=1),
        "lnE": np.stack([x["L1_xattn_ln1_w"], x["L1_xattn_ln1_b"], x["L1_xattn_ln2_w"], x["L1_xattn_ln2_b"]], axis=1),
        "gateF": cat([x["L1_ffn_gate"], x["L1_ffn_w_gate_s"][None]]).transpose(2, 0, 1),
        "upF": cat([x["L1_ffn_up"], x["L1_ffn_w_up_s"][None]]).transpose(2, 0, 1),
        "downF": cat([x["L1_ffn_down"], x["L1_ffn_w_down_s"][None]]).transpose(2, 0, 1).reshape(2, P, EXP + 1, P)
                 .transpose(1, 2, 0, 3),
    }
    arrays = {k: np.ascontiguousarray(v) for k, v in arrays.items()}
    nc = bacc.Bacc("TRN2", target_bir_lowering=False, num_devices=1)
    aps = {k: nc.dram_tensor(k + "_dram", v.shape, mybir.dt.from_np(v.dtype), kind="ExternalInput").ap()
           for k, v in arrays.items()}
    aps["out"] = nc.dram_tensor("out_dram", (BATCH, P, TT, P), F32, kind="ExternalOutput").ap()
    build(nc, aps)
    r = run_bass_kernel_spmd(nc, [{k + "_dram": v for k, v in arrays.items()}], core_ids=[0])
    out = r.results[0]["out_dram"]
    return np.ascontiguousarray(out.transpose(0, 2, 1, 3).reshape(BATCH, T, P))
```

```python
from contextlib import ExitStack

import concourse.bass as bass
from concourse import mybir

F32 = mybir.dt.float32
F32R = mybir.dt.float32r
U32 = mybir.dt.uint32
ALU = mybir.AluOpType
ACT = mybir.ActivationFunctionType
AX = mybir.AxisListType.X

P = 128
BATCH = 4
T = 512
TT = T // P
CTX = 77
HEADS = 16
DH = 64
INNER = HEADS * DH
NC = INNER // P
DB = P // HEADS
EXP = 8
HID = 256
KEYS = T + CTX
KPAD = 592
KPIECE = KPAD // 2
TILES = HEADS * TT
CPAD = CTX + 1
EPS = 1e-5
TH = T // HEADS


QK_IN = 16 * 4 * 5


def build(nc, a):
    with ExitStack() as ctx:
        def sb(name, shape, dt=F32):
            return ctx.enter_context(nc.sbuf_tensor(name, shape, dt))

        def sem(name):
            return ctx.enter_context(nc.semaphore(name))

        signals = []

        def sig(name):
            signals.append(sem(name))
            return signals[-1]

        def sigs(tag, names):
            return {n: sig(f"{n}_{tag}") for n in names.split()}

        ps = ctx.enter_context(nc.psum_tensor("ps", [P, 8, 512], F32))
        pair = [ps[:, 2 * i:2 * i + 2, :].rearrange("p b c -> p (b c)") for i in range(3)]
        OB, YB = ps[:, 6, :], ps[:, 7, :]

        ident, tok_eye, spread = sb("ident", [P, P]), sb("tok_eye", [P, TH]), sb("spread", [P, 4, P])
        head_mask, expert_no = sb("head_mask", [P, HEADS]), sb("expert_no", [P, EXP])
        neg_half = sb("neg_half", [P, TT])
        G = {n: (sb(f"g{n}_h", [P, HEADS, P], F32R), sb(f"g{n}_l", [P, HEADS, P], F32R)) for n in "AE"}
        split_w = {n: (sb(n + "_h", [P, w], F32R), sb(n + "_l", [P, w], F32R)) for n, w in
                   (("wvA", INNER), ("wvE", INNER), ("wqB", P), ("w1C", EXP * P), ("rC", EXP), ("wD", 3 * P), ("rF", EXP))}
        plain_w = {n: sb(n, s) for n, s in
                   (("woA", [P, NC, P]), ("woE", [P, NC, P]), ("wkB", [P, P]), ("wvB", [P, P]), ("woB", [P, P]),
                    ("w2C", [P, EXP, P]), ("woD", [P, P]), ("gateF", [P, EXP + 1, HID]), ("upF", [P, EXP + 1, HID]),
                    ("downF", [P, EXP + 1, 2, P]))}
        bqB, bkB, bD, lnE = sb("bqB", [P, 1]), sb("bkB", [P, 1]), sb("bD", [P, 3]), sb("lnE", [P, 4])
        rows_w = {n: sb(n, [P, w]) for n, w in (("bvB", P), ("boB", P), ("boD", P), ("biasC", EXP))}

        x_in, c_in, cz, cT = sb("x_in", [P, TT, P]), sb("c_in", [P, P]), sb("cz", [P, P]), sb("cT", [P, CTX])
        x0, x1, res = sb("x0", [P, TT, P]), sb("x1", [P, TT, P]), sb("res", [P, TT, P])
        keyh, keyl, key32 = sb("keyh", [P, KPAD], F32R), sb("keyl", [P, KPAD], F32R), sb("key32", [P, KPAD])
        xh, xl = keyh[:, 0:T], keyl[:, 0:T]
        stats, mv, veps, rstd = sb("stats", [P, TT, 6]), sb("mv", [P, TT, 2]), sb("veps", [P, TT]), sb("rstd", [P, TT])
        negm, sums, rec, diag = (sb(n, [P, TILES]) for n in ("negm", "sums", "rec", "diag"))
        lg, biased, top, idxf, oh1, oh2, tmp, comb = (sb(n, [P, TT, EXP]) for n in
                                                      ("lg", "biased", "top", "idxf", "oh1", "oh2", "tmp", "comb"))
        idx = sb("idx", [P, TT, 8], U32)
        gl, gm, gs, gr = sb("gl", [P, TT, 2]), sb("gm", [P, TT]), sb("gs", [P, TT]), sb("gr", [P, TT])

        AW, RW = 13056, 8192
        arena, arena_r = sb("arena", [P, AW]), sb("arena_r", [P, RW], F32R)

        def parts(base, *widths):
            at, out = 0, []
            for w in widths:
                out.append(base[:, at:at + w])
                at += w
            assert at <= base.shape[1], at
            return out

        raw = parts(arena, *[h.shape[1] for h, _ in split_w.values()], *[HEADS * P] * 4)
        raw_qk = [r.rearrange("p (h d) -> p h d", h=HEADS) for r in raw[len(split_w):]]
        V, *rest = parts(arena, 5 * INNER, *[T] * (NC - 1), *[KEYS] * 3, *[5 * P] * 4)
        V = V.rearrange("p (k n) -> p k n", k=5)
        ZT = rest[0:NC - 1] + [res[:].rearrange("p t d -> p (t d)")]
        pr, ptf = rest[NC - 1:NC + 2] + [key32[:, 0:KEYS]], rest[NC + 2:]
        pt = [v.rearrange("p (k q) -> p k q", k=5) for v in ptf]
        xT_in = arena[:, 5 * INNER:5 * INNER + T]
        ys = parts(arena_r, *[T] * 8)
        y_h, y_l = ys[0:4], ys[4:8]
        _, kb_h, kb_l = parts(arena_r, 8 * T, HEADS * CPAD, HEADS * CPAD)
        qb_h, qb_l = ys[0:2]
        kb = [v.rearrange("p (h j) -> p h j", h=HEADS) for v in (kb_h, kb_l)]
        k32, khB, klB = parts(x0[:].rearrange("p t d -> p (t d)"), CTX, CTX, CTX)
        v_b = x1[0:CTX].rearrange("p t d -> p (t d)")[:, 0:HEADS * (DB + 1)].rearrange("p (h d) -> p h d", h=HEADS)
        q32, aoB, aoT, xb, *pb = parts(arena, *[T] * 4, *[8 * CTX] * 4, *[8 * P] * 2)
        pb, pbtf = pb[0:4], pb[4:6]
        pb = [v.rearrange("p (h j) -> p h j", h=8) for v in pb]
        pbt = [v.rearrange("p (h q) -> p h q", h=8) for v in pbtf]
        h0, h1, silu0, silu1 = parts(arena, 2 * T, 2 * T, T, T)
        ht = [v.rearrange("p (c t) -> p c t", c=2) for v in (h0, h1)]
        silu = [silu0, silu1]
        QW = HEADS * P
        qk_parts = parts(arena_r, QW, QW, QW, QW)
        qs = [v.rearrange("p (c t) -> p c t", c=HEADS) for v in qk_parts[0:2]]
        ks = [v.rearrange("p (e c t) -> p e c t", e=4, c=HEADS) for v in qk_parts[2:4]]
        ex0, ex1, dg, qd, kd, vT, ovT, rr, *qk_hl = parts(arena, 4 * 640, 4 * 640, 4 * P, T, T, T, T, 4 * T, T, T, T, T)
        ex, dg, rr = [ex0, ex1], dg.rearrange("p (i q) -> p i q", i=4), rr.rearrange("p (i t) -> p i t", i=4)
        qk_scratch = nc.dram_tensor("qk_scratch", [4, P, T], F32, kind="Internal").ap()

        w_in, w_hi, w_lo = sem("weights_in"), sem("weights_hi"), sem("weights_lo")
        g_mm, g_hi, g_lo, const_ok = sem("g_product"), sem("g_hi"), sem("g_lo"), sem("constants_set")
        loaded, stored = sig("batch_loaded"), sig("out_stored")
        vstep = sig("vector_step")
        var_ok, rstd_ok, xn_ok = sig("variance_ready"), sig("rstd_ready"), sig("x_ready")
        xt_mm, xh_ok, xl_ok = sig("xT_product"), sig("xT_hi"), sig("xT_lo")
        key_ok = sig("keys_scaled")
        att = {n: sigs(n, "v_mm v_act v_dve y_mm y_hi y_lo score negmax prob norm tr pt pv z proj")
               for n in "AE"}
        B_ = sigs("B", "kv ksplit kb v q_mm q score sub prob tr pt pv ao aot_mm aot resid proj")
        C_ = sigs("C", "route gin gexp up act down acc")
        D_ = sigs("D", "zero qkv split scratch qk0 qk1 qk2 qk3 score negmax prob mask dsum r spread ov proj")
        F_ = sigs("F", "route up silu h down acc")

        loads = [(ident[:], a["ident"]), (tok_eye[:], a["tok_eye"]), (spread[:], a["spread"]),
                 (head_mask[:], a["head_mask"]), (expert_no[:], a["expert_no"])]
        loads += [(raw_qk[i][0:DH], a[n]) for i, n in enumerate(("wqA", "wkA", "wqE", "wkE"))]
        loads += [(raw[i], a[n]) for i, n in enumerate(split_w)]
        loads += [(t[:], a[n]) for n, t in plain_w.items()]
        loads += [(bqB[:], a["bqB"]), (bkB[:], a["bkB"]), (bD[:], a["bD"]), (lnE[:], a["lnE"])]
        loads += [(t[:], a[n].partition_broadcast(P)) for n, t in rows_w.items()]
        W_ALL = 16 * len(loads)
        def head_and_rows(i):
            return 2 * (i // (2 * TT)) + i % 2, i % (2 * TT) // 2

        setup = ctx.enter_context(ExitStack())
        block = setup.enter_context(nc.Block())

        @block.sync
        def _(sp):
            for dst, src in loads:
                sp.dma_start(dst, src).then_inc(w_in, 16)

        @block.gpsimd
        def _(pool):
            nc.gpsimd.memset(neg_half[:], -0.5).then_inc(const_ok, 1)


        @block.tensor
        def _(pe):
            pe.wait_ge(w_in, W_ALL)
            for i, n in enumerate("AE"):
                for h in range(HEADS):
                    pe.matmul(ps[:, 4 * i + h // 4, P * (h % 4):P * (h % 4) + P], raw_qk[2 * i][0:DH, h], raw_qk[2 * i + 1][0:DH, h],
                              start=True, stop=True).then_inc(g_mm, 1)

        @block.scalar
        def _(act):
            act.wait_ge(w_in, W_ALL)
            for (h, _), r in zip(split_w.values(), raw):
                nc.scalar.copy(h[:], r).then_inc(w_hi, 1)
            for i, n in enumerate("AE"):
                act.wait_ge(g_mm, HEADS * (i + 1))
                nc.scalar.mul(G[n][0][:].rearrange("p (b h) d -> p b (h d)", b=4), ps[:, 4 * i:4 * i + 4, :], DH ** -0.5
                              ).then_inc(g_hi, 1)


        @block.vector
        def _(dve):
            dve.wait_ge(w_in, W_ALL)
            nc.vector.memset(key32[:, KEYS:KPAD], 0.0).then_inc(const_ok, 1)
            for i, ((h, l), r) in enumerate(zip(split_w.values(), raw)):
                dve.wait_ge(w_hi, i + 1)
                nc.vector.tensor_tensor(l[:], r, h[:].bitcast(F32), ALU.subtract).then_inc(w_lo, 1)
            for i, n in enumerate("AE"):
                dve.wait_ge(g_hi, i + 1)
                for c in range(4):
                    g = [x[:, 4 * c:4 * c + 4, :].rearrange("p h d -> p (h d)") for x in G[n]]
                    ins = nc.vector.scalar_tensor_tensor(out=g[1], in0=ps[:, 4 * i + c, :], scalar=DH ** -0.5, in1=g[0].bitcast(F32),
                                                 op0=ALU.mult, op1=ALU.subtract)
                ins.then_inc(g_lo, 1)
            dve.wait_ge(g_lo, 2)
            nc.vector.memset(ps[:, 5, 0:P], 0.0).then_inc(const_ok, 1)


        setup.close()

        b = ctx.enter_context(nc.Fori(0, BATCH))
        body = ctx.enter_context(ExitStack())
        block = body.enter_context(nc.Block(no_gpsimd_drain=True))

        @block.sync
        def _(sp):
            one = bass.ds(b, 1)
            sp.dma_start(xT_in, a["xT"][one].rearrange("o p t -> (o p) t")).then_inc(loaded, 16)
            sp.dma_start(x_in[:], a["x"][one].rearrange("o p t d -> (o p) t d")).then_inc(loaded, 16)
            sp.dma_start(c_in[0:CTX], a["ctx"][one].rearrange("o p d -> (o p) d")).then_inc(loaded, 16)
            sp.dma_start(cT[:], a["cT"][one].rearrange("o p t -> (o p) t")).then_inc(loaded, 16)
            sp.wait_ge(D_["split"], 1)
            for i in range(4):
                sp.dma_start(qk_scratch[i], qk_hl[i]).then_inc(D_["scratch"], 16)
            sp.wait_ge(D_["zero"], 1)
            sp.wait_ge(D_["scratch"], 64)
            for u in range(4):
                if u >= 2:
                    sp.wait_ge(D_["score"], 4 * (u - 1))
                for row, (iq, ik) in enumerate(((0, 2), (1, 2), (0, 3), (1, 3))):
                    at = slice(DB * row, DB * row + DB)
                    src = qk_scratch[iq, :, u * P:(u + 1) * P].rearrange("(c x) t -> x c t", x=DB)
                    sp.dma_start(qs[u % 2][at].bitcast(F32), src).then_inc(D_[f"qk{u}"], 16)
                    for e in range(4):
                        src = qk_scratch[ik, :, u * P + TH * e:u * P + TH * e + TH].rearrange("(c x) t -> x c t", x=DB)
                        sp.dma_start(ks[u % 2][at, e].bitcast(F32), src).then_inc(D_[f"qk{u}"], 16)
            sp.wait_ge(xn_ok, 8)
            sp.dma_start(a["out"][one].rearrange("o p t d -> (o p) t d"), x1[:]).then_inc(stored, 16)
            sp.wait_ge(stored, 16)

        @block.gpsimd
        def _(pool):
            def inverse_root(b, k, rows=P, n=TT):
                pool.wait_ge(var_ok, k + 1)
                nc.gpsimd.tensor_tensor(rstd[0:rows, 0:n], veps[0:rows, 0:n], neg_half[0:rows, 0:n], ALU.pow).then_inc(rstd_ok, 1)

            pool.wait_ge(B_["ksplit"], 1)
            for x, src in zip(kb, (khB, klB)):
                ins = nc.gpsimd.tensor_tensor(x[:, :, 0:CTX], src[:, None, :].to_broadcast([P, HEADS, CTX]),
                                              head_mask[:][:, :, None].to_broadcast([P, HEADS, CTX]), ALU.mult)
            ins.then_inc(B_["kb"], 1)
            inverse_root(b, 0)
            pool.wait_ge(xn_ok, 1)
            nc.gpsimd.tensor_tensor(xb.rearrange("p (t d) -> p t d", t=TT), x0[:], rows_w["boB"][:][:, None, :].to_broadcast([P, TT, P]),
                                    ALU.add).then_inc(B_["resid"], 1)
            inverse_root(b, 1)
            pool.wait_ge(xn_ok, 2)
            nc.gpsimd.memset(arena_r[:].bitcast(F32), 0.0).then_inc(D_["zero"], 1)
            inverse_root(b, 2)
            for e in range(HEADS):
                pool.wait_ge(D_["prob"], 4 * e + 4)
                if e >= 1:
                    pool.wait_ge(D_["dsum"], e)
                v = ex[e % 2].rearrange("p (i k) -> p i k", k=640)[:, :, 0:P]
                nc.gpsimd.tensor_tensor(dg, v, ident[:, None, :].to_broadcast([P, 4, P]), ALU.mult).then_inc(D_["mask"], 1)
            inverse_root(b, 3)
            inverse_root(b, 4)
            inverse_root(b, 5, CTX, 1)
            inverse_root(b, 6)
            inverse_root(b, 7)

        @block.tensor
        def _(pe):
            def mm(out, lhsT, rhs, start=True, stop=True):
                return pe.matmul(out, lhsT, rhs, start=start, stop=stop, skip_group_check=True)

            def mm3(out, lhsT, rhs):
                (lh, ll), (rh, rl) = lhsT, rhs
                mm(out, lh, rh, stop=False)
                mm(out, lh, rl, start=False, stop=False)
                return mm(out, ll, rh, start=False)

            def cols(pieces, at):
                return [p[:, at] for p in pieces]

            XT = (xh, xl)
            tok = [slice(P * t, P * t + P) for t in range(TT)]

            def transpose_x(b, k, src, j):
                pe.wait_ge(xn_ok, k + 1)
                for t in range(TT):
                    ins = pe.transpose(YB[:, tok[t]], src[:, t], ident[:])
                ins.then_inc(xt_mm, 1)

            def attention(b, s, n, wv, nk, wo, kx):
                pe.wait_ge(xl_ok, kx)
                wv = split_w[wv]
                key = [slice(P * k, P * k + P) for k in range(TT)] + [slice(T, KEYS)]
                rows = [P] * TT + [CTX]
                for g in range(2 * nk):
                    k, half = divmod(g, 2)
                    if g >= 4:
                        pe.wait_ge(s["v_act"] if g % 2 == 0 else s["v_dve"], (g - 4) // 2 + 1)
                    mm3(ps[0:rows[k], g % 4, :], cols((keyh, keyl), key[k]),
                                     cols(wv, slice(512 * half, 512 * half + 512))).then_inc(s["v_mm"], 1)

                def mix_head(h):
                    if h >= 1:
                        pe.wait_ge(s["y_lo"], h)
                    mm3(YB, [g[:, h, :] for g in G[n]], XT).then_inc(s["y_mm"], 1)

                mix_head(0)
                mix_head(1)
                pe.wait_ge(s["v_act"], nk)
                pe.wait_ge(s["v_dve"], nk)
                for i in range(TILES + 6):
                    if i < TILES:
                        h, q = head_and_rows(i)
                        if i % (2 * TT) == 0:
                            pe.wait_ge(s["y_lo"], h + 2)
                        if i >= 2:
                            pe.wait_ge(s["prob"], i - 1)
                        lhsT = (y_h[h % 4][:, tok[q]], y_l[h % 4][:, tok[q]])
                        if nk == TT:
                            ins = mm3(pair[i % 2][:, 0:T], lhsT, XT)
                        else:
                            for w in range(2):
                                at = 512 - KPIECE + w * KPIECE
                                ins = mm3(pair[i % 2][:, at:at + KPIECE], lhsT,
                                          cols((keyh, keyl), slice(w * KPIECE, w * KPIECE + KPIECE)))
                        ins.then_inc(s["score"], 1)
                        if i % (2 * TT) in (0, 3) and h - h % 2 + 2 < HEADS:
                            mix_head(h - h % 2 + (2 if i % (2 * TT) == 0 else 3))
                    if i >= 6:
                        j = (i - 6) // 2 * 2
                        h, q = head_and_rows(j)
                        if i % 2 == 0:
                            pe.wait_ge(s["pt"], j + 2)
                            if q == 0 and h >= 2:
                                pe.wait_ge(s["z"], h // 2)
                        for k in range((nk + 1) // 2) if i % 2 == 0 else range((nk + 1) // 2, nk):
                            for hh in range(2):
                                ins = mm(ps[DH * hh:DH * hh + DH, 6, tok[q]],
                                         V[0:rows[k], k, DH * (h + hh):DH * (h + hh) + DH],
                                         pt[(j + hh) % 4][0:rows[k], k, :], start=k == 0, stop=k == nk - 1)
                        if i % 2 == 1:
                            ins.then_inc(s["pv"], 1)
                    if 3 <= i < TILES + 3:
                        j = i - 3
                        pe.wait_ge(s["norm"], j + 1)
                        if nk == TT:
                            bank = ps[:, 4 + j % 2, :]
                            if j >= 2:
                                pe.wait_ge(s["pt"], j - 1)
                        else:
                            bank = pair[2]
                            if j >= 1:
                                pe.wait_ge(s["pt"], j)
                        for k in range(nk):
                            ins = pe.transpose(bank[0:rows[k], P * k:P * k + P], pr[j % 4][:, key[k]], ident[:])
                        ins.then_inc(s["tr"], 1)
                pe.wait_ge(s["z"], NC)
                for q in range(TT):
                    for c in range(NC):
                        ins = mm(YB[:, tok[q]], ZT[c][:, tok[q]], plain_w[wo][:, c, :],
                                 start=c == 0, stop=c == NC - 1)
                ins.then_inc(s["proj"], 1)

            def project(b, s, ready, srcT, w, out):
                pe.wait_ge(ready, 1)
                for t in range(TT):
                    ins = mm(out[:, tok[t]], srcT[:, tok[t]], w[:])
                ins.then_inc(s["proj"], 1)

            def small_heads_kv(b):
                pe.wait_ge(loaded, 64)
                mm(ps[:, 4, 0:CTX], plain_w["wkB"][:], cT[:])
                mm(ps[0:CTX, 5, 0:P], cT[:], plain_w["wvB"][:]).then_inc(B_["kv"], 1)

            def small_heads(b):
                s = B_
                pe.wait_ge(xl_ok, 2)
                mm3(ps[:, 7, :], cols(split_w["wqB"], slice(0, P)), XT).then_inc(s["q_mm"], 1)
                pe.wait_ge(s["kb"], 1)
                pe.wait_ge(s["v"], 1)
                pe.wait_ge(s["q"], 1)
                for n in range(2 * TT + 3):
                    if n < 2 * TT:
                        i, half = divmod(n, 2)
                        if n >= 2:
                            pe.wait_ge(s["sub"], n - 1)
                        for g in (2 * half, 2 * half + 1):
                            at = slice(4 * CPAD * g, 4 * CPAD * (g + 1))
                            ins = mm3(ps[:, g, 0:4 * CPAD], (qb_h[:, tok[i]], qb_l[:, tok[i]]), (kb_h[:, at], kb_l[:, at]))
                        ins.then_inc(s["score"], 1)
                    m = n - 2
                    if 0 <= m < 2 * TT:
                        pe.wait_ge(s["prob"], m + 1)
                        for g in range(2):
                            if m >= 1:
                                pe.wait_ge(s["pt"], 2 * m + g - 1)
                            for h in range(4):
                                ins = pe.transpose(ps[0:CTX, 4 + g, P * h:P * h + P], pb[m % 4][:, 4 * g + h, :], ident[:])
                            ins.then_inc(s["tr"], 1)
                    m = n - 3
                    if m >= 0:
                        q, half = divmod(m, 2)
                        pe.wait_ge(s["pt"], 2 * m + 2)
                        if half == 0 and q >= 2:
                            pe.wait_ge(s["ao"], q - 1)
                        for h in range(8):
                            at = (DB + 1) * (8 * half + h)
                            ins = mm(ps[:, 6 + q % 2, at:at + DB + 1], pbt[m % 2][0:CTX, h, :], v_b[:, 8 * half + h, :])
                        ins.then_inc(s["pv"], 1)
                for t in range(TT):
                    pe.wait_ge(s["ao"], t + 1)
                    ins = pe.transpose(ps[:, 0, tok[t]], aoB[:, tok[t]], ident[:])
                ins.then_inc(s["aot_mm"], 1)
                project(b, s, s["aot"], aoT, plain_w["woB"], OB)

            def route(b, s, w, kx):
                pe.wait_ge(xl_ok, kx)
                for t in range(TT):
                    ins = mm3(YB[:, EXP * t:EXP * t + EXP], (xh[:, tok[t]], xl[:, tok[t]]), cols(split_w[w], slice(0, EXP)))
                ins.then_inc(s["route"], 1)

            def gelu_experts(b):
                s = C_
                route(b, s, "rC", 3)
                for e in range(EXP + 1):
                    if e < EXP:
                        if e >= 2:
                            pe.wait_ge(s["act"], e - 1)
                        mm3(ps[:, e % 2, :], cols(split_w["w1C"], slice(P * e, P * e + P)), XT).then_inc(s["up"], 1)
                    if e >= 1:
                        d = e - 1
                        pe.wait_ge(s["act"], e)
                        if d >= 2:
                            pe.wait_ge(s["acc"], d - 1)
                        for t in range(TT):
                            ins = mm(ps[:, 2 + d % 2, tok[t]], ht[d % 2][:, 0, tok[t]], plain_w["w2C"][:, d, :])
                        ins.then_inc(s["down"], 1)

            def diagonal_attention(b):
                s = D_
                pe.wait_ge(xl_ok, 4)
                for i in range(3):
                    mm3(ps[:, i, :], cols(split_w["wD"], slice(P * i, P * i + P)), XT).then_inc(s["qkv"], 1)
                for e in range(HEADS):
                    u = e // 4
                    if e % 4 == 0:
                        pe.wait_ge(s[f"qk{u}"], QK_IN)
                    if e >= 2:
                        pe.wait_ge(s["prob"], 4 * (e - 1))
                    for i in range(4):
                        ins = mm(ps[:, 4 * (e % 2) + i, :], ks[u % 2][:, e % 4, 4 * i:4 * i + 4, :].rearrange("p c t -> p (c t)"),
                                 qs[u % 2][:, :, TH * (e % 4):TH * (e % 4) + TH])
                    ins.then_inc(s["score"], 1)
                pe.wait_ge(s["r"], 1)
                for i in range(4):
                    ins = mm(ps[:, 0, :], spread[:, i, :], rr[:, i, :], start=i == 0, stop=i == 3)
                ins.then_inc(s["spread"], 1)
                project(b, s, s["ov"], ovT, plain_w["woD"], ps[:, 1, :])

            def swiglu_experts(b):
                s = F_
                route(b, s, "rF", 6)
                for j in range(2 * EXP + 4):
                    if j < 2 * EXP + 2:
                        e, c = divmod(j, 2)
                        if j >= 2:
                            pe.wait_ge(s["h"], j - 1)
                        mm(ps[:, 2 * (j % 2), :], plain_w["gateF"][:, e, P * c:P * c + P], key32[:, 0:T])
                        mm(ps[:, 2 * (j % 2) + 1, :], plain_w["upF"][:, e, P * c:P * c + P], key32[:, 0:T]).then_inc(s["up"], 1)
                    if j >= 3 and j % 2 == 1:
                        d = (j - 3) // 2
                        pe.wait_ge(s["h"], 2 * d + 2)
                        if d >= 2:
                            pe.wait_ge(s["acc"], d - 1)
                        for t in range(TT):
                            for c in range(2):
                                ins = mm(ps[:, 4 + d % 2, tok[t]], ht[d % 2][:, c, tok[t]], plain_w["downF"][:, d, c, :],
                                         start=c == 0, stop=c == 1)
                        ins.then_inc(s["down"], 1)

            small_heads_kv(b)
            attention(b, att["A"], "A", "wvA", TT, "woA", 1)
            transpose_x(b, 0, x0, 0)
            small_heads(b)
            transpose_x(b, 1, x1, 1)
            gelu_experts(b)
            transpose_x(b, 2, x0, 2)
            diagonal_attention(b)
            transpose_x(b, 4, x0, 3)
            pe.wait_ge(xn_ok, 6)
            pe.transpose(OB[:, 0:CTX], cz[0:CTX, :], ident[0:CTX, 0:CTX]).then_inc(xt_mm, 1)
            attention(b, att["E"], "E", "wvE", TT + 1, "woE", 5)
            transpose_x(b, 6, x0, 5)
            swiglu_experts(b)

        @block.scalar
        def _(act):
            def x_hi(b, j, src=None):
                if src is None:
                    act.wait_ge(xt_mm, j)
                    nc.scalar.copy(xh, YB).then_inc(xh_ok, 1)
                else:
                    nc.scalar.copy(keyh[:, 0:src.shape[1]], src).then_inc(xh_ok, 1)

            def attention(b, s, nk):
                rows = [P] * TT + [CTX]
                width = T if nk == TT else KEYS
                at = 0 if nk == TT else 512 - KPIECE
                for g in range(0, 2 * nk, 2):
                    k = g // 2
                    act.wait_ge(s["v_mm"], g + 1)
                    nc.scalar.copy(V[0:rows[k], k, 0:512], ps[0:rows[k], g % 4, :]).then_inc(s["v_act"], 1)

                def mix_hi(h):
                    act.wait_ge(s["y_mm"], h + 1)
                    nc.scalar.copy(y_h[h % 4], YB).then_inc(s["y_hi"], 1)

                mix_hi(0)
                mix_hi(1)
                for i in range(TILES + 3):
                    if i < TILES:
                        act.wait_ge(s["negmax"], i + 1)
                        if i >= 4:
                            act.wait_ge(s["tr"], i - 3)
                        nc.scalar.activation(pr[i % 4][:, 0:width], pair[i % 2][:, at:at + width], ACT.Exp,
                                             bias=negm[:, i:i + 1], accum_out=sums[:, i:i + 1]).then_inc(s["prob"], 1)
                    j = i - 3
                    if j >= 0:
                        act.wait_ge(s["tr"], j + 1)
                        if j >= 4:
                            act.wait_ge(s["pv"], (j - 4) // 2 + 1)
                        src = ps[:, 4 + j % 2, :] if nk == TT else pair[2][:, 0:P * nk]
                        nc.scalar.copy(ptf[j % 4][:, 0:P * nk], src).then_inc(s["pt"], 1)
                    h = i // (2 * TT) * 2 + 2
                    if i % (2 * TT) in (0, 3) and h < HEADS:
                        mix_hi(h if i % (2 * TT) == 0 else h + 1)

            act.wait_ge(loaded, 64)
            x_hi(b, 0, xT_in)
            attention(b, att["A"], TT)
            x_hi(b, 1)
            s = B_
            for n in range(2 * TT + 2):
                if n < 2 * TT:
                    act.wait_ge(s["sub"], n + 1)
                    nc.scalar.activation(pb[n % 4], pb[n % 4], ACT.Exp).then_inc(s["prob"], 1)
                m = n - 2
                if m >= 0:
                    if m >= 2:
                        act.wait_ge(s["pv"], m - 1)
                    for g in range(2):
                        act.wait_ge(s["tr"], 2 * m + g + 1)
                        nc.scalar.copy(pbtf[m % 2][0:CTX, 4 * P * g:4 * P * g + 4 * P], ps[0:CTX, 4 + g, :]).then_inc(s["pt"], 1)
            act.wait_ge(s["aot_mm"], 1)
            nc.scalar.copy(aoT, ps[:, 0, :]).then_inc(s["aot"], 1)
            x_hi(b, 2)
            s = C_
            act.wait_ge(s["gin"], 1)
            nc.scalar.activation(gl[:], gl[:], ACT.Exp).then_inc(s["gexp"], 1)
            for e in range(EXP):
                act.wait_ge(s["up"], e + 1)
                if e >= 2:
                    act.wait_ge(s["down"], e - 1)
                nc.scalar.activation(ht[e % 2][:, 0, :], ps[:, e % 2, :], ACT.Gelu).then_inc(s["act"], 1)
            x_hi(b, 3)
            s = D_
            for e in range(HEADS):
                act.wait_ge(s["negmax"], e + 1)
                if e >= 2:
                    act.wait_ge(s["mask"], e - 1)
                for i in range(4):
                    c = 4 * e + i
                    nc.scalar.activation(ex[e % 2][:, T * i:T * i + T], ps[:, 4 * (e % 2) + i, :], ACT.Exp,
                                                      bias=negm[:, c:c + 1], accum_out=sums[:, c:c + 1]).then_inc(s["prob"], 1)
            act.wait_ge(key_ok, 1)
            x_hi(b, 4, key32[:])
            attention(b, att["E"], TT + 1)
            x_hi(b, 6)
            s = F_
            for j in range(2 * EXP + 2):
                act.wait_ge(s["up"], j + 1)
                if j >= 2:
                    act.wait_ge(s["h"], j - 1)
                nc.scalar.activation(silu[j % 2], ps[:, 2 * (j % 2), :], ACT.Silu).then_inc(s["silu"], 1)

        @block.vector
        def _(dve):
            v = nc.vector
            steps = [0]

            def link(ins):
                steps[0] += 1
                ins.then_inc(vstep, 1)
                dve.wait_ge(vstep, steps[0])

            def over(t, shape, axis):
                at = [slice(None)] * t.ndim
                at.insert(axis, None)
                return t[tuple(at)].to_broadcast(shape)

            def norm(b, k, src, dst, rows=P, n=TT):
                for t in range(n):
                    ins = v.bn_stats(stats[0:rows, t, :], src[0:rows, t, :])
                link(ins)
                for t in range(n):
                    ins = v.bn_aggr(mv[0:rows, t, :], stats[0:rows, t, :])
                link(ins)
                v.tensor_scalar(veps[0:rows, 0:n], mv[0:rows, 0:n, 1], EPS, None, ALU.add).then_inc(var_ok, 1)
                dve.wait_ge(rstd_ok, k + 1)
                for t in range(n):
                    ins = v.tensor_scalar(dst[0:rows, t, :], src[0:rows, t, :], mv[0:rows, t, 0:1], rstd[0:rows, t:t + 1],
                                          ALU.subtract, ALU.mult)
                return ins.then_inc(xn_ok, 1)

            def x_lo(b, j, src=None, width=T, keep=False):
                dve.wait_ge(xh_ok, j)
                if keep:
                    v.tensor_copy(key32[:, 0:T], YB)
                v.tensor_tensor(keyl[:, 0:width], YB if src is None else src, keyh[:, 0:width].bitcast(F32),
                                         ALU.subtract).then_inc(xl_ok, 1)

            def attention(b, s, nk):
                rows = [P] * TT + [CTX]
                width = T if nk == TT else KEYS
                at = 0 if nk == TT else 512 - KPIECE
                for g in range(1, 2 * nk, 2):
                    k = g // 2
                    dve.wait_ge(s["v_mm"], g + 1)
                    v.tensor_copy(V[0:rows[k], k, 512:1024], ps[0:rows[k], g % 4, :]).then_inc(s["v_dve"], 1)

                def mix_lo(h):
                    dve.wait_ge(s["y_hi"], h + 1)
                    v.tensor_tensor(y_l[h % 4], YB, y_h[h % 4].bitcast(F32), ALU.subtract).then_inc(s["y_lo"], 1)

                mix_lo(0)
                mix_lo(1)
                for i in range(TILES + 6):
                    if i < TILES:
                        dve.wait_ge(s["score"], i + 1)
                        v.tensor_reduce(negm[:, i:i + 1], pair[i % 2][:, at:at + width], AX, ALU.max,
                                        negate=True).then_inc(s["negmax"], 1)
                    if i >= 2 * TT + 5 and i % (2 * TT) == 5:
                        c = i // (2 * TT) - 1
                        dve.wait_ge(s["pv"], TT * (c + 1))
                        v.tensor_copy(ZT[c], OB).then_inc(s["z"], 1)
                    if 1 <= i <= TILES:
                        j = i - 1
                        dve.wait_ge(s["prob"], j + 1)
                        link(v.reciprocal(rec[:, j:j + 1], sums[:, j:j + 1]))
                        v.tensor_scalar(pr[j % 4][:, 0:width], pr[j % 4][:, 0:width], rec[:, j:j + 1], None, ALU.mult
                                        ).then_inc(s["norm"], 1)
                        h = i // (2 * TT) * 2 + 2
                        if i % (2 * TT) in (1, 4) and h < HEADS:
                            mix_lo(h if i % (2 * TT) == 1 else h + 1)
                dve.wait_ge(s["proj"], 1)

            tiles = lambda t: t.rearrange("p (t d) -> p t d", t=TT)

            def small_heads_kv(b):
                s = B_
                dve.wait_ge(s["kv"], 1)
                for x in kb:
                    v.memset(x.bitcast(F32)[:, :, CTX:CPAD], 0.0)
                v.memset(v_b[:, :, DB:DB + 1], 1.0)
                link(v.tensor_scalar(k32, ps[:, 4, 0:CTX], bkB[:, 0:1], None, ALU.add))
                link(v.tensor_copy(khB.bitcast(F32R), k32))
                v.tensor_tensor(klB.bitcast(F32R), k32, khB, ALU.subtract).then_inc(s["ksplit"], 1)
                v.tensor_tensor(v_b[:, :, 0:DB], ps[0:CTX, 5, 0:P].rearrange("p (h d) -> p h d", h=HEADS),
                                rows_w["bvB"][0:CTX].rearrange("p (h d) -> p h d", h=HEADS), ALU.add).then_inc(s["v"], 1)

            def small_heads(b):
                s = B_
                dve.wait_ge(s["q_mm"], 1)
                link(v.tensor_scalar(q32, YB, bqB[:, 0:1], DB ** -0.5, ALU.add, ALU.mult))
                link(v.tensor_copy(qb_h, q32))
                v.tensor_tensor(qb_l, q32, qb_h.bitcast(F32), ALU.subtract).then_inc(s["q"], 1)
                for n in range(2 * TT + 4):
                    if n < 2 * TT:
                        half = n % 2
                        S = ps[:, 2 * half:2 * half + 2, 0:4 * CPAD].rearrange("p b (h j) -> p b h j", h=4)[:, :, :, 0:CTX]
                        m = negm[:, 8 * n:8 * n + 8].rearrange("p (b h) -> p b h", b=2)
                        dve.wait_ge(s["score"], n + 1)
                        link(v.tensor_reduce(m, S, AX, ALU.max))
                        if n >= 4:
                            dve.wait_ge(s["tr"], 2 * (n - 4) + 2)
                        v.tensor_tensor(pb[n % 4].rearrange("p (b h) j -> p b h j", b=2), S,
                                        over(m, [P, 2, 4, CTX], 3), ALU.subtract).then_inc(s["sub"], 1)
                    if n >= 5 and n % 2 == 1:
                        q = (n - 5) // 2
                        c = slice(HEADS * q, HEADS * q + HEADS)
                        dve.wait_ge(s["pv"], 2 * q + 2)
                        o = ps[:, 6 + q % 2, 0:HEADS * (DB + 1)].rearrange("p (h d) -> p h d", h=HEADS)
                        link(v.reciprocal(rec[:, c], o[:, :, DB]))
                        v.tensor_tensor(aoB[:, P * q:P * q + P].rearrange("p (h d) -> p h d", h=HEADS), o[:, :, 0:DB],
                                        over(rec[:, c], [P, HEADS, DB], 2), ALU.mult).then_inc(s["ao"], 1)
                dve.wait_ge(s["proj"], 1)

            def pick(b, scores):
                for t in range(TT):
                    ins = v.max(top[:, t, :], scores[:, t, :])
                link(ins)
                for t in range(TT):
                    ins = v.max_index(idx[:, t, :], top[:, t, :], scores[:, t, :])
                link(ins)
                link(v.tensor_copy(idxf[:], idx[:]))

            def one_hot(dst, n):
                return v.tensor_tensor(dst[:], over(expert_no[:], [P, TT, EXP], 1),
                                       idxf[:, :, n:n + 1].to_broadcast([P, TT, EXP]), ALU.is_equal)

            def accumulate(b, s, e, x, bank, weighted=True):
                dve.wait_ge(s["down"], e + 1)
                if e >= 1:
                    dve.wait_ge(s["acc"], e)
                for t in range(TT):
                    base = (x if e == 0 else res)[:, t, :]
                    o = ps[:, bank, P * t:P * t + P]
                    if weighted:
                        ins = v.scalar_tensor_tensor(out=res[:, t, :], in0=o, scalar=comb[:, t, e:e + 1], in1=base,
                                                     op0=ALU.mult, op1=ALU.add)
                    else:
                        ins = v.tensor_tensor(res[:, t, :], o, base, ALU.add)
                ins.then_inc(s["acc"], 1)

            def gelu_experts(b):
                s = C_
                dve.wait_ge(s["route"], 1)
                logits = YB[:, 0:TT * EXP].rearrange("p (t e) -> p t e", t=TT)
                v.tensor_copy(lg[:], logits)
                link(v.tensor_tensor(biased[:], logits, over(rows_w["biasC"][:], [P, TT, EXP], 1), ALU.add))
                pick(b, biased)
                one_hot(oh1, 0)
                link(one_hot(oh2, 1))
                for n, oh in enumerate((oh1, oh2)):
                    link(v.tensor_tensor(tmp[:], lg[:], oh[:], ALU.mult))
                    link(v.tensor_reduce(gl[:, :, n:n + 1], tmp[:], AX, ALU.add))
                link(v.tensor_reduce(gm[:], gl[:], AX, ALU.max))
                v.tensor_tensor(gl[:], gl[:], over(gm[:], [P, TT, 2], 2), ALU.subtract).then_inc(s["gin"], 1)
                dve.wait_ge(s["gexp"], 1)
                link(v.tensor_reduce(gs[:], gl[:], AX, ALU.add))
                link(v.reciprocal(gr[:], gs[:]))
                link(v.tensor_tensor(gl[:], gl[:], over(gr[:], [P, TT, 2], 2), ALU.mult))
                v.tensor_tensor(comb[:], oh1[:], gl[:, :, 0:1].to_broadcast([P, TT, EXP]), ALU.mult)
                link(v.tensor_tensor(tmp[:], oh2[:], gl[:, :, 1:2].to_broadcast([P, TT, EXP]), ALU.mult))
                link(v.tensor_tensor(comb[:], comb[:], tmp[:], ALU.add))
                for e in range(EXP):
                    accumulate(b, s, e, x1, 2 + e % 2)
                dve.wait_ge(s["acc"], EXP)

            def diagonal_attention(b):
                s = D_
                for i, (dst, scale) in enumerate(((qd, P ** -0.5), (kd, P ** -0.5), (vT, None))):
                    dve.wait_ge(s["qkv"], i + 1)
                    link(v.tensor_scalar(dst, ps[:, i, :], bD[:, i:i + 1], *((scale, ALU.add, ALU.mult) if scale else
                                                                               (None, ALU.add))))
                for i, src in enumerate((qd, kd)):
                    link(v.tensor_copy(qk_hl[2 * i].bitcast(F32R), src))
                    ins = v.tensor_tensor(qk_hl[2 * i + 1].bitcast(F32R), src, qk_hl[2 * i], ALU.subtract)
                ins.then_inc(s["split"], 1)
                for e in range(HEADS + 1):
                    if e < HEADS:
                        dve.wait_ge(s["score"], e + 1)
                        v.tensor_reduce(negm[:, 4 * e:4 * e + 4], ps[:, 4 * (e % 2):4 * (e % 2) + 4, :], AX,
                                                       ALU.max, negate=True).then_inc(s["negmax"], 1)
                    if e >= 1:
                        dve.wait_ge(s["mask"], e)
                        v.tensor_reduce(diag[:, 4 * e - 4:4 * e], dg, AX, ALU.add).then_inc(s["dsum"], 1)
                link(v.reciprocal(rec[:], sums[:]))
                link(v.tensor_tensor(diag[:], diag[:], rec[:], ALU.mult))
                by_chunk = diag[:].rearrange("p (e i) -> p i e", i=4)
                for i in range(4):
                    ins = v.tensor_tensor(rr[:, i, :].rearrange("p (e t) -> p e t", e=HEADS),
                                          over(by_chunk[:, i, :], [P, HEADS, TH], 2), over(tok_eye[:], [P, HEADS, TH], 1),
                                          ALU.mult)
                ins.then_inc(s["r"], 1)
                dve.wait_ge(s["spread"], 1)
                v.tensor_tensor(ovT, ps[:, 0, :], vT, ALU.mult).then_inc(s["ov"], 1)
                dve.wait_ge(s["proj"], 1)

            def swiglu_experts(b):
                s = F_
                dve.wait_ge(s["route"], 1)
                link(v.tensor_copy(lg[:], YB[:, 0:TT * EXP].rearrange("p (t e) -> p t e", t=TT)))
                pick(b, lg)
                link(one_hot(comb, 0))
                for j in range(2 * EXP + 2):
                    e, c = divmod(j, 2)
                    dve.wait_ge(s["silu"], j + 1)
                    if e >= 2 and c == 0:
                        dve.wait_ge(s["down"], e - 1)
                    v.tensor_tensor(ht[e % 2][:, c, :], ps[:, 2 * (j % 2) + 1, :], silu[j % 2], ALU.mult).then_inc(s["h"], 1)
                    if c == 1 and e >= 1:
                        accumulate(b, s, e - 1, x0, 4 + (e - 1) % 2)
                accumulate(b, s, EXP, x0, 4 + EXP % 2, weighted=False)
                dve.wait_ge(s["acc"], EXP + 1)

            dve.wait_ge(loaded, 64)
            x_lo(b, 1, xT_in)
            small_heads_kv(b)
            attention(b, att["A"], TT)
            link(v.scalar_tensor_tensor(out=res[:], in0=x_in[:], scalar=2.0, in1=tiles(YB), op0=ALU.mult, op1=ALU.add))
            norm(b, 0, res, x0)
            x_lo(b, 2)
            small_heads(b)
            dve.wait_ge(B_["resid"], 1)
            link(v.tensor_tensor(res[:], tiles(OB), tiles(xb), ALU.add))
            norm(b, 1, res, x1)
            x_lo(b, 3)
            gelu_experts(b)
            norm(b, 2, res, x0)
            x_lo(b, 4)
            diagonal_attention(b)
            link(v.tensor_tensor(res[:], tiles(ps[:, 1, :]), over(rows_w["boD"][:], [P, TT, P], 1), ALU.add))
            link(v.tensor_tensor(res[:], res[:], x0[:], ALU.add))
            norm(b, 3, res, x1)
            dve.wait_ge(xn_ok, 4)
            norm(b, 4, x1, x0)
            dve.wait_ge(xn_ok, 5)
            norm(b, 5, c_in[:].rearrange("p (o d) -> p o d", o=1), cz[:].rearrange("p (o d) -> p o d", o=1), CTX, 1)
            dve.wait_ge(xt_mm, 4)
            v.tensor_scalar(key32[:, 0:T], YB, lnE[:, 2:3], lnE[:, 3:4], ALU.mult, ALU.add)
            dve.wait_ge(xt_mm, 5)
            v.tensor_scalar(key32[:, T:KEYS], OB[:, 0:CTX], lnE[:, 0:1], lnE[:, 1:2], ALU.mult, ALU.add).then_inc(key_ok, 1)
            x_lo(b, 5, key32[:], KPAD)
            attention(b, att["E"], TT + 1)
            link(v.tensor_tensor(res[:], tiles(YB), x1[:], ALU.add))
            norm(b, 6, res, x0)
            x_lo(b, 6, keep=True)
            swiglu_experts(b)
            norm(b, 7, res, x1)

        body.close()
        numbers = [s.num for s in signals]
        assert numbers == list(range(numbers[0], numbers[0] + len(numbers)))
        nc.sync.sem_clear(range(numbers[0], numbers[-1] + 1))
        nc.all_engine_barrier()


def kernel(**inputs):
    import numpy as np
    import concourse.bacc as bacc
    from concourse.bass_utils import run_bass_kernel_spmd

    x = {k: np.ascontiguousarray(v) for k, v in inputs.items()}
    f32 = np.float32
    cat = np.concatenate

    def by_head(w):
        return w.transpose(2, 1, 0)

    def out_proj(w):
        return w.reshape(NC, P, P).transpose(1, 0, 2)

    wkv = x["L1_xattn_Wkv"]
    part, col = np.arange(P), np.arange(P)
    spread = np.zeros((P, 4, P), f32)
    for i in range(4):
        spread[:, i, :] = col[None, :] // DB == 4 * i + part[:, None] // TH
    arrays = {
        "xT": x["x"].transpose(0, 2, 1), "x": x["x"].reshape(BATCH, TT, P, P).transpose(0, 2, 1, 3),
        "ctx": x["ctx_1024"], "cT": x["ctx_1024"].transpose(0, 2, 1),
        "ident": np.eye(P, dtype=f32), "spread": spread,
        "tok_eye": (part[:, None] % TH == np.arange(TH)[None, :]).astype(f32),
        "head_mask": (part[:, None] // DB == np.arange(HEADS)[None, :]).astype(f32),
        "expert_no": np.tile(np.arange(EXP, dtype=f32), (P, 1)),
        "wqA": by_head(x["L0_attn_w_q"].transpose(1, 0, 2)), "wkA": by_head(x["L0_attn_w_k"].transpose(1, 0, 2)),
        "wqE": by_head(x["L1_xattn_Wq"].reshape(P, HEADS, DH)), "wkE": by_head(wkv[:, :INNER].reshape(P, HEADS, DH)),
        "wvA": x["L0_attn_w_v"].transpose(1, 0, 2).reshape(P, INNER), "wvE": wkv[:, INNER:],
        "woA": out_proj(x["L0_attn_w_o"]), "woE": out_proj(x["L1_xattn_Wo"]),
        "wqB": x["L0_xattn_wq"], "wkB": x["L0_xattn_wk"], "wvB": x["L0_xattn_wv"], "woB": x["L0_xattn_wo"],
        "bqB": x["L0_xattn_bq"].reshape(P, 1), "bkB": x["L0_xattn_bk"].reshape(P, 1),
        "bvB": x["L0_xattn_bv"], "boB": x["L0_xattn_bo"], "boD": x["L1_attn_b_o"], "biasC": x["L0_ffn_auxfree_bias"],
        "w1C": x["L0_ffn_w1"].transpose(2, 0, 1).reshape(P, EXP * P), "w2C": x["L0_ffn_w2"].transpose(2, 0, 1),
        "rC": x["L0_ffn_router_w"].T, "rF": x["L1_ffn_router"].T,
        "wD": cat([x["L1_attn_W_q"], x["L1_attn_W_k"], x["L1_attn_W_v"]], axis=1), "woD": x["L1_attn_W_o"],
        "bD": np.stack([x["L1_attn_b_q"], x["L1_attn_b_k"], x["L1_attn_b_v"]], axis=1),
        "lnE": np.stack([x["L1_xattn_ln1_w"], x["L1_xattn_ln1_b"], x["L1_xattn_ln2_w"], x["L1_xattn_ln2_b"]], axis=1),
        "gateF": cat([x["L1_ffn_gate"], x["L1_ffn_w_gate_s"][None]]).transpose(2, 0, 1),
        "upF": cat([x["L1_ffn_up"], x["L1_ffn_w_up_s"][None]]).transpose(2, 0, 1),
        "downF": cat([x["L1_ffn_down"], x["L1_ffn_w_down_s"][None]]).transpose(2, 0, 1).reshape(2, P, EXP + 1, P)
                 .transpose(1, 2, 0, 3),
    }
    arrays = {k: np.ascontiguousarray(v) for k, v in arrays.items()}
    nc = bacc.Bacc("TRN2", target_bir_lowering=False, num_devices=1)
    aps = {k: nc.dram_tensor(k + "_dram", v.shape, mybir.dt.from_np(v.dtype), kind="ExternalInput").ap()
           for k, v in arrays.items()}
    aps["out"] = nc.dram_tensor("out_dram", (BATCH, P, TT, P), F32, kind="ExternalOutput").ap()
    build(nc, aps)
    r = run_bass_kernel_spmd(nc, [{k + "_dram": v for k, v in arrays.items()}], core_ids=[0])
    out = r.results[0]["out_dram"]
    return np.ascontiguousarray(out.transpose(0, 2, 1, 3).reshape(BATCH, T, P))
```

```python
import math
from contextlib import ExitStack

import concourse.bass as bass
from concourse import mybir

F32 = mybir.dt.float32
F32R = mybir.dt.float32r
U32 = mybir.dt.uint32
ALU = mybir.AluOpType
ACT = mybir.ActivationFunctionType
AX = mybir.AxisListType.X

P = 128
BATCH = 4
T = 512
TT = T // P
CTX = 77
HEADS = 16
DH = 64
INNER = HEADS * DH
NC = INNER // P
DB = P // HEADS
EXP = 8
HID = 256
KEYS = T + CTX
KPAD = 592
KPIECE = KPAD // 2
TILES = HEADS * TT
CPAD = CTX + 1
EPS = 1e-5
TH = T // HEADS



def build(nc, a):
    with ExitStack() as ctx:
        def sb(name, shape, dt=F32):
            return ctx.enter_context(nc.sbuf_tensor(name, shape, dt))

        def sem(name):
            return ctx.enter_context(nc.semaphore(name))

        signals = []

        def sig(name):
            signals.append(sem(name))
            return signals[-1]

        def sigs(tag, names):
            return {n: sig(f"{n}_{tag}") for n in names.split()}

        ps = ctx.enter_context(nc.psum_tensor("ps", [P, 8, 512], F32))
        pair = [ps[:, 2 * i:2 * i + 2, :].rearrange("p b c -> p (b c)") for i in range(3)]
        OB, YB = ps[:, 6, :], ps[:, 7, :]

        ident, tok_eye, spread = sb("ident", [P, P]), sb("tok_eye", [P, TH]), sb("spread", [P, 4, P])
        head_mask, expert_no = sb("head_mask", [P, HEADS]), sb("expert_no", [P, EXP])
        neg_half, euler = sb("neg_half", [P, TT]), sb("euler", [P, TT, 2])
        G = {n: (sb(f"g{n}_h", [P, HEADS, P], F32R), sb(f"g{n}_l", [P, HEADS, P], F32R)) for n in "AE"}
        split_w = {n: (sb(n + "_h", [P, w], F32R), sb(n + "_l", [P, w], F32R)) for n, w in
                   (("wvA", INNER), ("wvE", INNER), ("wqB", P), ("w1C", EXP * P), ("wD", 3 * P))}
        plain_w = {n: sb(n, s) for n, s in
                   (("woA", [P, NC, P]), ("woE", [P, NC, P]), ("wkB", [P, P]), ("wvB", [P, P]), ("woB", [P, P]),
                    ("w2C", [P, EXP, P]), ("woD", [P, P]), ("gateF", [P, EXP + 1, HID]), ("upF", [P, EXP + 1, HID]),
                    ("downF", [P, EXP + 1, 2, P]), ("rC", [P, EXP]), ("rF", [P, EXP]))}
        bqB, bkB, bD, lnE = sb("bqB", [P, 1]), sb("bkB", [P, 1]), sb("bD", [P, 3]), sb("lnE", [P, 4])
        rows_w = {n: sb(n, [P, w]) for n, w in (("bvB", P), ("boB", P), ("boD", P), ("biasC", EXP))}

        x_in, c_in, cz, cT = sb("x_in", [P, TT, P]), sb("c_in", [P, P]), sb("cz", [P, P]), sb("cT", [P, CTX])
        x0, x1, res = sb("x0", [P, TT, P]), sb("x1", [P, TT, P]), sb("res", [P, TT, P])
        keyh, keyl, key32 = sb("keyh", [P, KPAD], F32R), sb("keyl", [P, KPAD], F32R), sb("key32", [P, KPAD])
        xh, xl = keyh[:, 0:T], keyl[:, 0:T]
        stats, mv, veps, rstd = sb("stats", [P, TT, 6]), sb("mv", [P, TT, 2]), sb("veps", [P, TT]), sb("rstd", [P, TT])
        negm, sums, rec, diag = (sb(n, [P, TILES]) for n in ("negm", "sums", "rec", "diag"))
        lg, biased, top, idxf, oh1, oh2, tmp, comb = (sb(n, [P, TT, EXP]) for n in
                                                      ("lg", "biased", "top", "idxf", "oh1", "oh2", "tmp", "comb"))
        idx = sb("idx", [P, TT, 8], U32)
        gl, gm, gs, gr = sb("gl", [P, TT, 2]), sb("gm", [P, TT]), sb("gs", [P, TT]), sb("gr", [P, TT])

        v_b = sb("v_b", [CTX, P])
        v_m = x1[:].rearrange("p t d -> p (t d)").rearrange("p (h m) -> p h m", h=HEADS)

        AW, RW = 13031, 8192
        arena, arena_r = sb("arena", [P, AW]), sb("arena_r", [P, RW], F32R)

        def parts(base, *widths):
            at, out = 0, []
            for w in widths:
                out.append(base[:, at:at + w])
                at += w
            assert at <= base.shape[1], at
            return out

        raw = parts(arena, *[h.shape[1] for h, _ in split_w.values()], *[HEADS * P] * 4)
        raw_qk = [r.rearrange("p (h d) -> p h d", h=HEADS) for r in raw[len(split_w):]]
        V, *rest = parts(arena, 5 * INNER, *[T] * (NC - 1), *[KEYS] * 3, *[5 * P] * 4)
        V = V.rearrange("p (k n) -> p k n", k=5)
        ZT = rest[0:NC - 1] + [res[:].rearrange("p t d -> p (t d)")]
        pr, ptf = rest[NC - 1:NC + 2] + [key32[:, 0:KEYS]], rest[NC + 2:]
        pt = [v.rearrange("p (k q) -> p k q", k=5) for v in ptf]
        xT_in = arena[:, AW - T:]
        ys = parts(arena_r, *[T] * 8)
        y_h, y_l = ys[0:4], ys[4:8]
        _, kb_h, kb_l = parts(arena_r, 8 * T, HEADS * CPAD, HEADS * CPAD)
        qb_h, qb_l = ys[0:2]
        kb = [v.rearrange("p (h j) -> p h j", h=HEADS) for v in (kb_h, kb_l)]
        k32, khB, klB = parts(x0[:].rearrange("p t d -> p (t d)"), CTX, CTX, CTX)
        q32, aoT, xb, *pb = parts(arena, *[T] * 3, *[8 * CTX] * 4, *[8 * P] * 2)
        pb, pbtf = pb[0:4], pb[4:6]
        pb = [v.rearrange("p (h j) -> p h j", h=8) for v in pb]
        pbt = [v.rearrange("p (h q) -> p h q", h=8) for v in pbtf]
        h0, h1, silu0, silu1 = parts(arena, 2 * T, 2 * T, T, T)
        ht = [v.rearrange("p (c t) -> p c t", c=2) for v in (h0, h1)]
        silu = [silu0, silu1]
        QW = HEADS * P
        qk_parts = parts(arena_r, QW, QW, QW, QW)
        qs = [v.rearrange("p (c t) -> p c t", c=HEADS) for v in qk_parts[0:2]]
        ks = [v.rearrange("p (e c t) -> p e c t", e=4, c=HEADS) for v in qk_parts[2:4]]
        ex0, ex1, dg0, dg1, qd, kd, vT, ovT, rr, xd, *qk_hl = parts(arena, 4 * 640, 4 * 640, *[4 * P] * 2, *[T] * 4, 4 * T, *[T] * 5)
        ex, dg, rr = [ex0, ex1], [v.rearrange("p (i q) -> p i q", i=4) for v in (dg0, dg1)], rr.rearrange("p (i t) -> p i t", i=4)
        q_scratch = [nc.dram_tensor(f"q_scratch{n}", [2, DB, quarters, HEADS, P], F32, kind="Internal").ap()
                     for n, quarters in enumerate((1, 3))]
        k_scratch = [nc.dram_tensor(f"k_scratch{n}", [2, DB, quarters, 4, HEADS, TH], F32, kind="Internal").ap()
                     for n, quarters in enumerate((1, 3))]

        def weights_spread(u):
            shape = [P, 4, 4, TH]
            out = rr[:, :, P * u:P * u + P].rearrange("p i (e t) -> p i e t", e=4)
            w = diag[:, 16 * u:16 * u + 16].rearrange("p (e i) -> p i e", i=4)
            return out, w[:, :, :, None].to_broadcast(shape), tok_eye[:][:, None, None, :].to_broadcast(shape)

        first_in, plain_in, w_hi, w_lo = sem("first_in"), sem("plain_weights_in"), sem("weights_hi"), sem("weights_lo")
        mix_in = [sem("wqk_A_in"), sem("wqk_E_in")]
        split_in = {n: sem(n + "_in") for n in split_w}
        g_mm, g_hi, g_lo, const_ok = sem("g_product"), sem("g_hi"), sem("g_lo"), sem("constants_set")
        last_stored = sem("last_out_stored")
        loaded, stored = sig("batch_loaded"), sig("out_stored")
        vstep = sig("vector_step")
        var_ok, rstd_ok, xn_ok = sig("variance_ready"), sig("rstd_ready"), sig("x_ready")
        x32_ok = sig("xT_copied")
        xt_mm, xh_ok, xl_ok = sig("xT_product"), sig("xT_hi"), sig("xT_lo")
        key_ok = sig("keys_scaled")
        att = {n: sigs(n, "v_mm v_act v_dve y_mm y_hi y_lo score negmax prob norm tr pt pv z proj")
               for n in "AE"}
        B_ = sigs("B", "kv ksplit kb v vzero vm q_mm q score sub prob rec norm tr pt pv aot resid proj")
        C_ = sigs("C", "route gin gexp up act down acc")
        D_ = sigs("D", "fold resid zero qkv qk32 hi lo scratch0 scratch1 qk0 qk1 qk2 qk3 score negmax prob mask dsum rec w v r r_last spread ov proj")
        F_ = sigs("F", "route up silu h down acc")

        mix_loads = [[(raw_qk[2 * i + j][0:DH], a[w + n]) for j, w in enumerate(("wq", "wk"))] for i, n in enumerate("AE")]
        split_loads = [(raw[i], a[n]) for i, n in enumerate(split_w)]
        small = ("wkB", "wvB")
        first_loads = [(head_mask[:], a["head_mask"]), (bkB[:], a["bkB"]), (bqB[:], a["bqB"]), (bD[:], a["bD"]), (lnE[:], a["lnE"]),
                       (ident[:], a["ident"]), (tok_eye[:], a["tok_eye"]), (expert_no[:], a["expert_no"])]
        first_loads += [(t[:], a[n].partition_broadcast(P)) for n, t in rows_w.items()]
        first_loads += [(plain_w[n][:], a[n]) for n in small]
        plain_loads = [(t[:], a[n]) for n, t in plain_w.items() if n not in small] + [(spread[:], a["spread"])]

        def batch_inputs(one):
            return [(xT_in, a["xT"][one].rearrange("o p t -> (o p) t")),
                    (x_in[:], a["x"][one].rearrange("o p t d -> (o p) t d")),
                    (c_in[0:CTX], a["ctx"][one].rearrange("o p d -> (o p) d")),
                    (cT[:], a["cT"][one].rearrange("o p t -> (o p) t"))]

        first_loads += batch_inputs(slice(BATCH - 1, BATCH))
        PLAIN_IN = 16 * len(plain_loads)

        def normed(k):
            return 1 + TT * k

        def half_normed(k, half):
            return 2 * k + half if k else 1

        def head_and_rows(i):
            return 2 * (i // (2 * TT)) + i % 2, i % (2 * TT) // 2

        setup = ctx.enter_context(ExitStack())
        block = setup.enter_context(nc.Block())

        @block.sync
        def _(sp):
            for i in range(2):
                for dst, src in mix_loads[i]:
                    sp.dma_start(dst, src).then_inc(mix_in[i], 16)
            for (dst, src), name in zip(split_loads, split_w):
                sp.dma_start(dst, src).then_inc(split_in[name], 16)
            for dst, src in first_loads:
                sp.dma_start(dst, src).then_inc(first_in, 16)
            for dst, src in plain_loads:
                sp.dma_start(dst, src).then_inc(plain_in, 16)

        @block.gpsimd
        def _(pool):
            nc.gpsimd.memset(neg_half[:], -0.5).then_inc(const_ok, 1)
            nc.gpsimd.memset(euler[:], math.e).then_inc(const_ok, 1)

        @block.tensor
        def _(pe):
            for i, n in enumerate("AE"):
                pe.wait_ge(mix_in[i], 32)
                for h in range(HEADS):
                    pe.matmul(ps[:, 4 * i + h // 4, P * (h % 4):P * (h % 4) + P], raw_qk[2 * i][0:DH, h], raw_qk[2 * i + 1][0:DH, h],
                              start=True, stop=True).then_inc(g_mm, 1)

        @block.scalar
        def _(act):
            for i, n in enumerate("AE"):
                act.wait_ge(g_mm, HEADS * (i + 1))
                nc.scalar.mul(G[n][0][:].rearrange("p (b h) d -> p b (h d)", b=4), ps[:, 4 * i:4 * i + 4, :], DH ** -0.5
                              ).then_inc(g_hi, 1)
            for n, r in zip(split_w, raw):
                act.wait_ge(split_in[n], 16)
                nc.scalar.copy(split_w[n][0][:], r).then_inc(w_hi, 1)
            act.wait_ge(first_in, 16 * len(first_loads))

        @block.vector
        def _(dve):
            nc.vector.memset(key32[:, KEYS:KPAD], 0.0).then_inc(const_ok, 1)
            nc.vector.memset(x1[:], 0.0).then_inc(const_ok, 1)
            nc.vector.memset(arena[DH:P, 4 * INNER:5 * INNER], 0.0).then_inc(const_ok, 1)
            for i, n in enumerate("AE"):
                dve.wait_ge(g_hi, i + 1)
                for c in range(4):
                    g = [x[:, 4 * c:4 * c + 4, :].rearrange("p h d -> p (h d)") for x in G[n]]
                    ins = nc.vector.scalar_tensor_tensor(out=g[1], in0=ps[:, 4 * i + c, :], scalar=DH ** -0.5, in1=g[0].bitcast(F32),
                                                 op0=ALU.mult, op1=ALU.subtract)
                ins.then_inc(g_lo, 1)
            for i, ((h, l), r) in enumerate(zip(split_w.values(), raw)):
                dve.wait_ge(w_hi, i + 1)
                nc.vector.tensor_tensor(l[:], r, h[:].bitcast(F32), ALU.subtract).then_inc(w_lo, 1)
            dve.wait_ge(g_lo, 2)
            nc.vector.memset(ps[:, 5, 0:P], 0.0).then_inc(const_ok, 1)

        setup.close()

        loop = ctx.enter_context(ExitStack())
        b = loop.enter_context(nc.Fori(0, BATCH))
        body = ctx.enter_context(ExitStack())
        block = body.enter_context(nc.Block(no_gpsimd_drain=True))

        @block.sync
        def _(sp):
            one = bass.ds(b, 1)
            sp.dma_start(a["out"][one].rearrange("o p t d -> (o p) t d"), x1[:]).then_inc(stored, 16)
            for i in range(2):
                sp.wait_ge(D_["hi"] if i == 0 else D_["lo"], 1)
                sp.dma_start(q_scratch[0][i].rearrange("x u c t -> c x u t"), qk_hl[i][:, 0:P]).then_inc(D_["scratch0"], 16)
            for i in range(2):
                sp.wait_ge(D_["hi"] if i == 0 else D_["lo"], 2)
                sp.dma_start(k_scratch[0][i].rearrange("x u e c t -> c x (u e) t"), qk_hl[2 + i][:, 0:P]).then_inc(D_["scratch0"], 16)
            for i in range(2):
                sp.dma_start(q_scratch[1][i].rearrange("x u c t -> c x u t"), qk_hl[i][:, P:T]).then_inc(D_["scratch1"], 16)
            sp.wait_ge(D_["zero"], 1)
            sp.wait_ge(D_["scratch0"], 16 * 4)
            for u in range(4):
                if u == 1:
                    for i in range(2):
                        sp.dma_start(k_scratch[1][i].rearrange("x u e c t -> c x (u e) t"), qk_hl[2 + i][:, P:T]
                                     ).then_inc(D_["scratch1"], 16)
                    sp.wait_ge(D_["scratch1"], 16 * 4)
                if u >= 2:
                    sp.wait_ge(D_["score"], 8 * (u - 1))
                part, at = min(u, 1), max(u - 1, 0)
                src = q_scratch[part][:, :, at].rearrange("n x c t -> (n x) (c t)")[None].to_broadcast([2, 2 * DB, QW])
                sp.dma_start(qk_parts[u % 2][0:4 * DB].bitcast(F32), src).then_inc(D_[f"qk{u}"], 16)
                for n in range(2):
                    src = k_scratch[part][n, :, at].rearrange("x e c t -> x (e c t)")[None].to_broadcast([2, DB, QW])
                    sp.dma_start(qk_parts[2 + u % 2][2 * DB * n:2 * DB * n + 2 * DB].bitcast(F32), src).then_inc(D_[f"qk{u}"], 16)
            sp.wait_ge(xn_ok, normed(6))
            for dst, src in batch_inputs(one):
                sp.dma_start(dst, src).then_inc(loaded, 16)
            sp.wait_ge(loaded, 64)
            sp.wait_ge(stored, 16)

        @block.gpsimd
        def _(pool):
            def inverse_roots(b, k):
                for half in range(2 if k else 1):
                    rows, t = (P, slice(2 * half, 2 * half + 2)) if k else (CTX, slice(0, 1))
                    pool.wait_ge(var_ok, half_normed(k, half))
                    nc.gpsimd.tensor_tensor(rstd[0:rows, t], veps[0:rows, t], neg_half[0:rows, t], ALU.pow).then_inc(rstd_ok, 1)

            pool.wait_ge(B_["ksplit"], 1)
            for x, src in zip(kb, (khB, klB)):
                ins = nc.gpsimd.tensor_tensor(x[:, :, 0:CTX], src[:, None, :].to_broadcast([P, HEADS, CTX]),
                                              head_mask[:][:, :, None].to_broadcast([P, HEADS, CTX]), ALU.mult)
            ins.then_inc(B_["kb"], 1)
            inverse_roots(b, 0)
            pool.wait_ge(stored, 16)
            nc.gpsimd.memset(v_m, 0.0).then_inc(B_["vzero"], 1)
            pool.wait_ge(B_["vzero"], 1)
            pool.wait_ge(B_["v"], 1)
            for l in range(4):
                ins = nc.gpsimd.tensor_copy(v_m[0:CTX, 4 * l:4 * l + 4, DB * l:DB * l + DB],
                                            v_b[:, TH * l:TH * l + TH].rearrange("p (g d) -> p g d", g=4))
            ins.then_inc(B_["vm"], 1)
            inverse_roots(b, 1)
            pool.wait_ge(xn_ok, normed(1))
            nc.gpsimd.tensor_tensor(xb.rearrange("p (t d) -> p t d", t=TT), x0[:], rows_w["boB"][:][:, None, :].to_broadcast([P, TT, P]),
                                    ALU.add).then_inc(B_["resid"], 1)
            for n in range(2 * TT):
                pool.wait_ge(B_["rec"], n + 1)
                nc.gpsimd.tensor_tensor(pb[n % 4], pb[n % 4], rec[:, 8 * n:8 * n + 8][:, :, None].to_broadcast([P, 8, CTX]),
                                        ALU.mult).then_inc(B_["norm"], 1)
            inverse_roots(b, 2)
            pool.wait_ge(C_["gin"], 1)
            nc.gpsimd.tensor_tensor(gl[:], euler[:], gl[:], ALU.pow).then_inc(C_["gexp"], 1)
            pool.wait_ge(xn_ok, normed(2))
            nc.gpsimd.memset(arena_r[:].bitcast(F32), 0.0).then_inc(D_["zero"], 1)
            inverse_roots(b, 3)
            pool.wait_ge(xn_ok, normed(3))
            nc.gpsimd.tensor_tensor(xd.rearrange("p (t d) -> p t d", t=TT), x0[:],
                                    rows_w["boD"][:][:, None, :].to_broadcast([P, TT, P]), ALU.add).then_inc(D_["resid"], 1)
            for e in range(HEADS):
                pool.wait_ge(D_["prob"], 4 * e + 4)
                if e >= 2:
                    pool.wait_ge(D_["dsum"], e - 1)
                v = ex[e % 2].rearrange("p (i k) -> p i k", k=640)[:, :, 0:P]
                nc.gpsimd.tensor_tensor(dg[e % 2], v, ident[:, None, :].to_broadcast([P, 4, P]), ALU.mult).then_inc(D_["mask"], 1)
                pool.wait_ge(D_["mask"], e + 1)
                half = dg[e % 2][:, :, 0:P // 2]
                nc.gpsimd.tensor_tensor(half, half, dg[e % 2][:, :, P // 2:P], ALU.add).then_inc(D_["fold"], 1)
                if e % 4 == 1 and e > 1:
                    u = (e - 5) // 4
                    c = slice(16 * u, 16 * u + 16)
                    pool.wait_ge(D_["rec"], u + 1)
                    nc.gpsimd.tensor_tensor(diag[:, c], diag[:, c], rec[:, c], ALU.mult).then_inc(D_["w"], 1)
                    pool.wait_ge(D_["w"], u + 1)
                    nc.gpsimd.tensor_tensor(*weights_spread(u), ALU.mult).then_inc(D_["r"], 1)
            inverse_roots(b, 4)
            inverse_roots(b, 5)
            inverse_roots(b, 6)
            inverse_roots(b, 7)

        @block.tensor
        def _(pe):
            def mm(out, lhsT, rhs, start=True, stop=True):
                return pe.matmul(out, lhsT, rhs, start=start, stop=stop, skip_group_check=True)

            def mm3(out, lhsT, rhs):
                (lh, ll), (rh, rl) = lhsT, rhs
                mm(out, lh, rh, stop=False)
                mm(out, lh, rl, start=False, stop=False)
                return mm(out, ll, rh, start=False)

            def cols(pieces, at):
                return [p[:, at] for p in pieces]

            XT = (xh, xl)
            tok = [slice(P * t, P * t + P) for t in range(TT)]

            def stay_warm(n, bank=0):
                for _ in range(n):
                    mm(ps[:, bank, :], split_w["wqB"][0][:], split_w["w1C"][0][:, 0:512])

            def transpose_x(b, k, src, idle):
                stay_warm(idle)
                for t in range(TT):
                    pe.wait_ge(xn_ok, normed(k - 1) + t + 1)
                    ins = pe.transpose(YB[:, tok[t]], src[:, t], ident[:])
                ins.then_inc(xt_mm, 1)

            def attention(b, s, n, wv, nk, wo, kx):
                pe.wait_ge(xl_ok, kx)
                wv = split_w[wv]
                key = [slice(P * k, P * k + P) for k in range(TT)] + [slice(T, KEYS)]
                rows = [P] * TT + [CTX]
                def mix_head(h):
                    if h >= 1:
                        pe.wait_ge(s["y_lo"], h)
                    mm3(YB, [g[:, h, :] for g in G[n]], XT).then_inc(s["y_mm"], 1)

                def project_chunk(c):
                    for q in range(TT):
                        ins = mm(YB[:, tok[q]], ZT[c][:, tok[q]], plain_w[wo][:, c, :], start=c == 0 and q == 0, stop=c == NC - 1)
                    return ins

                mix_head(0)
                for g in range(2 * nk):
                    k, half = divmod(g, 2)
                    if g == 4:
                        mix_head(1)
                    if g >= 4:
                        pe.wait_ge(s["v_act"] if g % 2 == 0 else s["v_dve"], (g - 4) // 2 + 1)
                    mm3(ps[0:rows[k], 2 + g % 4, :], cols((keyh, keyl), key[k]),
                                     cols(wv, slice(512 * half, 512 * half + 512))).then_inc(s["v_mm"], 1)
                for i in range(TILES + 6):
                    if i < TILES:
                        h, q = head_and_rows(i)
                        if i % (2 * TT) == 0:
                            pe.wait_ge(s["y_lo"], h + 2)
                        if i == 0 and nk == TT:
                            pe.wait_ge(B_["v"], 1)
                        if i == 1:
                            pe.wait_ge(s["v_act"], nk)
                            pe.wait_ge(s["v_dve"], nk)
                        if i >= 2:
                            pe.wait_ge(s["prob"], i - 1)
                        lhsT = (y_h[h % 4][:, tok[q]], y_l[h % 4][:, tok[q]])
                        if nk == TT:
                            ins = mm3(pair[i % 2][:, 0:T], lhsT, XT)
                        else:
                            for w in range(2):
                                at = 512 - KPIECE + w * KPIECE
                                ins = mm3(pair[i % 2][:, at:at + KPIECE], lhsT,
                                          cols((keyh, keyl), slice(w * KPIECE, w * KPIECE + KPIECE)))
                        ins.then_inc(s["score"], 1)
                        if i % (2 * TT) in (0, 3) and h - h % 2 + 2 < HEADS:
                            mix_head(h - h % 2 + (2 if i % (2 * TT) == 0 else 3))
                    if i >= TILES:
                        if i == TILES:
                            pe.wait_ge(plain_in, PLAIN_IN)
                        pe.wait_ge(s["z"], i - TILES + 2)
                        for c in (0, 1) if i == TILES else (i - TILES + 1,):
                            project_chunk(c)
                    if i >= 6:
                        j = (i - 6) // 2 * 2
                        h, q = head_and_rows(j)
                        if i % 2 == 0:
                            pe.wait_ge(s["pt"], j + 2)
                            if q == 0 and h >= 2:
                                pe.wait_ge(s["z"], h // 2)
                        for k in range((nk + 1) // 2) if i % 2 == 0 else range((nk + 1) // 2, nk):
                            for hh in range(2):
                                ins = mm(ps[DH * hh:DH * hh + DH, 6, tok[q]],
                                         V[0:rows[k], k, DH * (h + hh):DH * (h + hh) + DH],
                                         pt[(j + hh) % 4][0:rows[k], k, :], start=k == 0, stop=k == nk - 1)
                        if i % 2 == 1:
                            ins.then_inc(s["pv"], 1)
                    if 3 <= i < TILES + 3:
                        j = i - 3
                        pe.wait_ge(s["norm"], j + 1)
                        if nk == TT:
                            bank = ps[:, 4 + j % 2, :]
                            if j >= 2:
                                pe.wait_ge(s["pt"], j - 1)
                        else:
                            bank = pair[2]
                            if j >= 1:
                                pe.wait_ge(s["pt"], j)
                        for k in range(nk):
                            ins = pe.transpose(bank[0:rows[k], P * k:P * k + P], pr[j % 4][:, key[k]], ident[:])
                        ins.then_inc(s["tr"], 1)
                pe.wait_ge(s["z"], NC)
                ins = project_chunk(NC - 1)
                ins.then_inc(s["proj"], 1)

            def project(b, s, ready, srcT, w, out):
                pe.wait_ge(ready, 1)
                for t in range(TT):
                    ins = mm(out[:, tok[t]], srcT[:, tok[t]], w[:])
                ins.then_inc(s["proj"], 1)

            def small_heads_kv(b):
                mm(ps[:, 0, 0:CTX], plain_w["wkB"][:], cT[:])
                mm(ps[0:CTX, 1, 0:P], cT[:], plain_w["wvB"][:]).then_inc(B_["kv"], 1)

            def small_heads(b):
                s = B_
                pe.wait_ge(xl_ok, 2)
                mm3(ps[:, 7, :], cols(split_w["wqB"], slice(0, P)), XT).then_inc(s["q_mm"], 1)
                stay_warm(8)
                pe.wait_ge(s["kb"], 1)
                pe.wait_ge(s["vm"], 1)
                pe.wait_ge(s["q"], 1)
                for n in range(2 * TT + 4):
                    if n < 2 * TT:
                        i, half = divmod(n, 2)
                        if n >= 2:
                            pe.wait_ge(s["sub"], n - 1)
                        for g in (2 * half, 2 * half + 1):
                            at = slice(4 * CPAD * g, 4 * CPAD * (g + 1))
                            ins = mm3(ps[:, g, 0:4 * CPAD], (qb_h[:, tok[i]], qb_l[:, tok[i]]), (kb_h[:, at], kb_l[:, at]))
                        ins.then_inc(s["score"], 1)
                    m = n - 3
                    if m == 0:
                        stay_warm(8, 6)
                    if 0 <= m < 2 * TT:
                        pe.wait_ge(s["norm"], m + 1)
                        for g in range(2):
                            if m >= 1:
                                pe.wait_ge(s["pt"], 2 * m + g - 1)
                            for h in range(4):
                                ins = pe.transpose(ps[0:CTX, 4 + g, P * h:P * h + P], pb[m % 4][:, 4 * g + h, :], ident[:])
                            ins.then_inc(s["tr"], 1)
                    m = n - 4
                    if m >= 0:
                        q, half = divmod(m, 2)
                        pe.wait_ge(s["pt"], 2 * m + 2)
                        for l in (2 * half, 2 * half + 1):
                            for g in range(4):
                                ins = mm(OB[TH * g:TH * g + TH, tok[q]], v_m[:, 4 * l + g, :], pbt[m % 2][:, 4 * (l - 2 * half) + g, :],
                                         start=l == 0, stop=l == 3)
                        ins.then_inc(s["pv"], 1)
                project(b, s, s["aot"], aoT, plain_w["woB"], YB)

            def route(b, s, w):
                for t in range(TT):
                    ins = mm(YB[:, EXP * t:EXP * t + EXP], key32[:, tok[t]], plain_w[w][:])
                ins.then_inc(s["route"], 1)

            def gelu_experts(b):
                s = C_
                pe.wait_ge(x32_ok, 1)
                route(b, s, "rC")
                pe.wait_ge(xl_ok, 3)
                for e in range(EXP + 1):
                    if e < EXP:
                        if e >= 2:
                            pe.wait_ge(s["act"], e - 1)
                        mm3(ps[:, e % 2, :], cols(split_w["w1C"], slice(P * e, P * e + P)), XT).then_inc(s["up"], 1)
                    if e >= 1:
                        d = e - 1
                        pe.wait_ge(s["act"], e)
                        if d >= 4:
                            pe.wait_ge(s["acc"], d - 3)
                        for t in range(TT):
                            ins = mm(ps[:, 2 + d % 4, tok[t]], ht[d % 2][:, 0, tok[t]], plain_w["w2C"][:, d, :])
                        ins.then_inc(s["down"], 1)

            def diagonal_attention(b):
                s = D_
                pe.wait_ge(xl_ok, 4)
                for i in range(3):
                    mm3(ps[:, i, :], cols(split_w["wD"], slice(P * i, P * i + P)), XT).then_inc(s["qkv"], 1)
                for e in range(HEADS):
                    u = e // 4
                    if e % 4 == 0:
                        pe.wait_ge(s[f"qk{u}"], 48)
                    if e == 0:
                        pe.wait_ge(s["v"], 1)
                    for i in range(4):
                        if e >= 2:
                            pe.wait_ge(s["prob"], 4 * (e - 2) + i + 1)
                        ins = mm(ps[:, 4 * (e % 2) + i, :], ks[u % 2][:, e % 4, 4 * i:4 * i + 4, :].rearrange("p c t -> p (c t)"),
                                 qs[u % 2][:, :, TH * (e % 4):TH * (e % 4) + TH])
                        if i % 2 == 1:
                            ins.then_inc(s["score"], 1)
                pe.wait_ge(s["prob"], 4 * (HEADS - 1))
                pe.wait_ge(s["r"], 3)
                for u in range(TT):
                    if u == TT - 1:
                        pe.wait_ge(s["r_last"], 1)
                    for i in range(4):
                        ins = mm(ps[:, 0 if u < TT - 1 else 2, tok[u]], spread[:, i, :], rr[:, i, tok[u]], start=i == 0, stop=i == 3)
                    if u >= TT - 2:
                        ins.then_inc(s["spread"], 1)
                for t in range(TT):
                    pe.wait_ge(s["ov"], 1 if t < TT - 1 else 2)
                    ins = mm(ps[:, 1, tok[t]], ovT[:, tok[t]], plain_w["woD"][:])
                ins.then_inc(s["proj"], 1)

            def swiglu_experts(b):
                s = F_
                pe.wait_ge(x32_ok, 2)
                for j in range(2 * EXP + 4):
                    if j == 2:
                        route(b, s, "rF")
                    if j < 2 * EXP + 2:
                        e, c = divmod(j, 2)
                        if j >= 2:
                            pe.wait_ge(s["h"], j - 1)
                        mm(ps[:, 2 * (j % 2), :], plain_w["gateF"][:, e, P * c:P * c + P], key32[:, 0:T])
                        mm(ps[:, 2 * (j % 2) + 1, :], plain_w["upF"][:, e, P * c:P * c + P], key32[:, 0:T]).then_inc(s["up"], 1)
                    if j >= 3 and j % 2 == 1:
                        d = (j - 3) // 2
                        pe.wait_ge(s["h"], 2 * d + 2)
                        if d >= 2:
                            pe.wait_ge(s["acc"], d - 1)
                        for t in range(TT):
                            for c in range(2):
                                ins = mm(ps[:, 4 + d % 2, tok[t]], ht[d % 2][:, c, tok[t]], plain_w["downF"][:, d, c, :],
                                         start=c == 0, stop=c == 1)
                        ins.then_inc(s["down"], 1)

            small_heads_kv(b)
            stay_warm(2, 2)
            attention(b, att["A"], "A", "wvA", TT, "woA", 1)
            transpose_x(b, 1, x0, 22)
            small_heads(b)
            transpose_x(b, 2, x1, 18)
            gelu_experts(b)
            transpose_x(b, 3, x0, 22)
            diagonal_attention(b)
            stay_warm(16)
            pe.wait_ge(xn_ok, normed(0))
            pe.transpose(OB[:, 0:CTX], cz[0:CTX, :], ident[0:CTX, 0:CTX]).then_inc(xt_mm, 1)
            transpose_x(b, 5, x0, 11)
            attention(b, att["E"], "E", "wvE", TT + 1, "woE", 5)
            transpose_x(b, 6, x0, 20)
            swiglu_experts(b)
            stay_warm(18)

        @block.scalar
        def _(act):
            def x_hi(b, j, src=None):
                if src is None:
                    act.wait_ge(xt_mm, j)
                    nc.scalar.copy(xh, YB).then_inc(xh_ok, 1)
                else:
                    nc.scalar.copy(keyh[:, 0:src.shape[1]], src).then_inc(xh_ok, 1)

            def attention(b, s, nk):
                rows = [P] * TT + [CTX]
                width = T if nk == TT else KEYS
                at = 0 if nk == TT else 512 - KPIECE
                def mix_hi(h):
                    act.wait_ge(s["y_mm"], h + 1)
                    nc.scalar.copy(y_h[h % 4], YB).then_inc(s["y_hi"], 1)

                mix_hi(0)
                for g in range(0, 2 * nk, 2):
                    k = g // 2
                    if g == 4:
                        mix_hi(1)
                    act.wait_ge(s["v_mm"], g + 1)
                    nc.scalar.copy(V[0:rows[k], k, 0:512], ps[0:rows[k], 2 + g % 4, :]).then_inc(s["v_act"], 1)
                for i in range(TILES + 3):
                    if i < TILES:
                        act.wait_ge(s["negmax"], i + 1)
                        if i >= 4:
                            act.wait_ge(s["tr"], i - 3)
                        nc.scalar.activation(pr[i % 4][:, 0:width], pair[i % 2][:, at:at + width], ACT.Exp,
                                             bias=negm[:, i:i + 1], accum_out=sums[:, i:i + 1]).then_inc(s["prob"], 1)
                    j = i - 3
                    if j >= 0:
                        act.wait_ge(s["tr"], j + 1)
                        if j >= 4:
                            act.wait_ge(s["pv"], (j - 4) // 2 + 1)
                        src = ps[:, 4 + j % 2, :] if nk == TT else pair[2][:, 0:P * nk]
                        nc.scalar.copy(ptf[j % 4][:, 0:P * nk], src).then_inc(s["pt"], 1)
                    h = i // (2 * TT) * 2 + 2
                    if i % (2 * TT) in (0, 3) and h < HEADS:
                        mix_hi(h if i % (2 * TT) == 0 else h + 1)

            attention(b, att["A"], TT)
            x_hi(b, 1)
            s = B_
            for n in range(2 * TT + 3):
                if n < 2 * TT:
                    act.wait_ge(s["sub"], n + 1)
                    nc.scalar.activation(pb[n % 4], pb[n % 4], ACT.Exp).then_inc(s["prob"], 1)
                m = n - 3
                if m >= 0:
                    if m >= 2:
                        act.wait_ge(s["pv"], m - 1)
                    for g in range(2):
                        act.wait_ge(s["tr"], 2 * m + g + 1)
                        nc.scalar.copy(pbtf[m % 2][0:CTX, 4 * P * g:4 * P * g + 4 * P], ps[0:CTX, 4 + g, :]).then_inc(s["pt"], 1)
            act.wait_ge(s["pv"], 2 * TT)
            nc.scalar.copy(aoT, OB).then_inc(s["aot"], 1)
            act.wait_ge(x32_ok, 1)
            x_hi(b, 2, key32[:, 0:T])
            s = C_
            for e in range(EXP):
                act.wait_ge(s["up"], e + 1)
                if e >= 2:
                    act.wait_ge(s["down"], e - 1)
                nc.scalar.activation(ht[e % 2][:, 0, :], ps[:, e % 2, :], ACT.Gelu).then_inc(s["act"], 1)
            x_hi(b, 3)
            s = D_
            for i, src in enumerate((qd, kd)):
                act.wait_ge(s["qk32"], i + 1)
                nc.scalar.copy(qk_hl[2 * i].bitcast(F32R), src).then_inc(s["hi"], 1)
            for e in range(HEADS):
                if e >= 2:
                    act.wait_ge(s["mask"], e - 1)
                for i in range(4):
                    if i % 2 == 0:
                        act.wait_ge(s["negmax"], 2 * e + i // 2 + 1)
                    c = 4 * e + i
                    nc.scalar.activation(ex[e % 2][:, T * i:T * i + T], ps[:, 4 * (e % 2) + i, :], ACT.Exp,
                                                      bias=negm[:, c:c + 1], accum_out=sums[:, c:c + 1]).then_inc(s["prob"], 1)
            act.wait_ge(key_ok, 1)
            x_hi(b, 4, key32[:])
            attention(b, att["E"], TT + 1)
            s = F_
            for j in range(2 * EXP + 2):
                act.wait_ge(s["up"], j + 1)
                if j >= 2:
                    act.wait_ge(s["h"], j - 1)
                nc.scalar.activation(silu[j % 2], ps[:, 2 * (j % 2), :], ACT.Silu).then_inc(s["silu"], 1)

        @block.vector
        def _(dve):
            v = nc.vector
            steps = [0]

            def link(ins):
                steps[0] += 1
                ins.then_inc(vstep, 1)
                dve.wait_ge(vstep, steps[0])

            def over(t, shape, axis):
                at = [slice(None)] * t.ndim
                at.insert(axis, None)
                return t[tuple(at)].to_broadcast(shape)

            def norm(b, k, src, dst, rows=P, n=TT):
                halves = [slice(0, 2), slice(2, 4)] if n == TT else [slice(0, n)]
                stats_done = []
                for h in halves:
                    for t in range(h.start, h.stop):
                        ins = v.bn_stats(stats[0:rows, t, :], src[0:rows, t, :])
                    ins.then_inc(vstep, 1)
                    steps[0] += 1
                    stats_done.append(steps[0])
                for i, h in enumerate(halves):
                    dve.wait_ge(vstep, stats_done[i])
                    for t in range(h.start, h.stop):
                        ins = v.bn_aggr(mv[0:rows, t, :], stats[0:rows, t, :])
                    ins.then_inc(vstep, 1)
                    steps[0] += 1
                    dve.wait_ge(vstep, steps[0])
                    v.tensor_scalar(veps[0:rows, h], mv[0:rows, h, 1], EPS, None, ALU.add).then_inc(var_ok, 1)
                for i, h in enumerate(halves):
                    dve.wait_ge(rstd_ok, half_normed(k, i))
                    if k == 2 and i == 0:
                        dve.wait_ge(stored, 16)
                    for t in range(h.start, h.stop):
                        v.tensor_scalar(dst[0:rows, t, :], src[0:rows, t, :], mv[0:rows, t, 0:1], rstd[0:rows, t:t + 1],
                                        ALU.subtract, ALU.mult).then_inc(xn_ok, 1)

            def x_copy(b, k):
                dve.wait_ge(xt_mm, k)
                v.tensor_copy(key32[:, 0:T], YB).then_inc(x32_ok, 1)

            def x_lo(b, j, src=None, width=T):
                dve.wait_ge(xh_ok, j)
                v.tensor_tensor(keyl[:, 0:width], YB if src is None else src, keyh[:, 0:width].bitcast(F32),
                                         ALU.subtract).then_inc(xl_ok, 1)

            def attention(b, s, nk):
                rows = [P] * TT + [CTX]
                width = T if nk == TT else KEYS
                at = 0 if nk == TT else 512 - KPIECE
                def mix_lo(h):
                    dve.wait_ge(s["y_hi"], h + 1)
                    v.tensor_tensor(y_l[h % 4], YB, y_h[h % 4].bitcast(F32), ALU.subtract).then_inc(s["y_lo"], 1)

                mix_lo(0)
                for g in range(1, 2 * nk, 2):
                    k = g // 2
                    if g == 5:
                        mix_lo(1)
                    dve.wait_ge(s["v_mm"], g + 1)
                    v.tensor_copy(V[0:rows[k], k, 512:1024], ps[0:rows[k], 2 + g % 4, :]).then_inc(s["v_dve"], 1)
                for i in range(TILES + 6):
                    if i < TILES:
                        dve.wait_ge(s["score"], i + 1)
                        v.tensor_reduce(negm[:, i:i + 1], pair[i % 2][:, at:at + width], AX, ALU.max,
                                        negate=True).then_inc(s["negmax"], 1)
                    if i >= 2 * TT + 5 and i % (2 * TT) == 5:
                        c = i // (2 * TT) - 1
                        dve.wait_ge(s["pv"], TT * (c + 1))
                        v.tensor_copy(ZT[c], OB).then_inc(s["z"], 1)
                    if i == 2 * TT and nk == TT:
                        norm(b, 0, c_in[:].rearrange("p (o d) -> p o d", o=1), cz[:].rearrange("p (o d) -> p o d", o=1), CTX, 1)
                    if 1 <= i <= TILES:
                        j = i - 1
                        dve.wait_ge(s["prob"], j + 1)
                        link(v.reciprocal(rec[:, j:j + 1], sums[:, j:j + 1]))
                        v.tensor_scalar(pr[j % 4][:, 0:width], pr[j % 4][:, 0:width], rec[:, j:j + 1], None, ALU.mult
                                        ).then_inc(s["norm"], 1)
                        h = i // (2 * TT) * 2 + 2
                        if i % (2 * TT) in (1, 4) and h < HEADS:
                            mix_lo(h if i % (2 * TT) == 1 else h + 1)
                dve.wait_ge(s["proj"], 1)

            tiles = lambda t: t.rearrange("p (t d) -> p t d", t=TT)

            def small_heads_kv(b):
                s = B_
                dve.wait_ge(s["kv"], 1)
                for x in kb:
                    v.memset(x.bitcast(F32)[:, :, CTX:CPAD], 0.0)
                link(v.tensor_scalar(k32, ps[:, 0, 0:CTX], bkB[:, 0:1], None, ALU.add))
                link(v.tensor_copy(khB.bitcast(F32R), k32))
                v.tensor_tensor(klB.bitcast(F32R), k32, khB, ALU.subtract).then_inc(s["ksplit"], 1)
                v.tensor_tensor(v_b[:], ps[0:CTX, 1, 0:P], rows_w["bvB"][0:CTX], ALU.add).then_inc(s["v"], 1)

            def small_heads(b):
                s = B_
                dve.wait_ge(s["q_mm"], 1)
                link(v.tensor_scalar(q32, YB, bqB[:, 0:1], DB ** -0.5, ALU.add, ALU.mult))
                link(v.tensor_copy(qb_h, q32))
                v.tensor_tensor(qb_l, q32, qb_h.bitcast(F32), ALU.subtract).then_inc(s["q"], 1)
                for n in range(2 * TT + 1):
                    if n < 2 * TT:
                        half = n % 2
                        S = ps[:, 2 * half:2 * half + 2, 0:4 * CPAD].rearrange("p b (h j) -> p b h j", h=4)[:, :, :, 0:CTX]
                        m = negm[:, 8 * n:8 * n + 8].rearrange("p (b h) -> p b h", b=2)
                        dve.wait_ge(s["score"], n + 1)
                        link(v.tensor_reduce(m, S, AX, ALU.max))
                        if n >= 4:
                            dve.wait_ge(s["tr"], 2 * (n - 4) + 2)
                        v.tensor_tensor(pb[n % 4].rearrange("p (b h) j -> p b h j", b=2), S,
                                        over(m, [P, 2, 4, CTX], 3), ALU.subtract).then_inc(s["sub"], 1)
                    if n >= 1:
                        c = slice(8 * n - 8, 8 * n)
                        dve.wait_ge(s["prob"], n)
                        link(v.tensor_reduce(sums[:, c], pb[(n - 1) % 4], AX, ALU.add))
                        v.reciprocal(rec[:, c], sums[:, c]).then_inc(s["rec"], 1)
                dve.wait_ge(s["proj"], 1)

            def pick(b, scores):
                for t in range(TT):
                    ins = v.max(top[:, t, :], scores[:, t, :])
                link(ins)
                for t in range(TT):
                    ins = v.max_index(idx[:, t, :], top[:, t, :], scores[:, t, :])
                link(ins)
                link(v.tensor_copy(idxf[:], idx[:]))

            def one_hot(dst, n):
                return v.tensor_tensor(dst[:], over(expert_no[:], [P, TT, EXP], 1),
                                       idxf[:, :, n:n + 1].to_broadcast([P, TT, EXP]), ALU.is_equal)

            def accumulate(b, s, e, x, bank, weighted=True):
                dve.wait_ge(s["down"], e + 1)
                if e >= 1:
                    dve.wait_ge(s["acc"], e)
                for t in range(TT):
                    base = (x if e == 0 else res)[:, t, :]
                    o = ps[:, bank, P * t:P * t + P]
                    if weighted:
                        ins = v.scalar_tensor_tensor(out=res[:, t, :], in0=o, scalar=comb[:, t, e:e + 1], in1=base,
                                                     op0=ALU.mult, op1=ALU.add)
                    else:
                        ins = v.tensor_tensor(res[:, t, :], o, base, ALU.add)
                ins.then_inc(s["acc"], 1)

            def gelu_experts(b):
                s = C_
                dve.wait_ge(s["route"], 1)
                logits = YB[:, 0:TT * EXP].rearrange("p (t e) -> p t e", t=TT)
                v.tensor_copy(lg[:], logits)
                link(v.tensor_tensor(biased[:], logits, over(rows_w["biasC"][:], [P, TT, EXP], 1), ALU.add))
                pick(b, biased)
                one_hot(oh1, 0)
                link(one_hot(oh2, 1))
                for n, oh in enumerate((oh1, oh2)):
                    link(v.tensor_tensor(tmp[:], lg[:], oh[:], ALU.mult))
                    link(v.tensor_reduce(gl[:, :, n:n + 1], tmp[:], AX, ALU.add))
                link(v.tensor_reduce(gm[:], gl[:], AX, ALU.max))
                v.tensor_tensor(gl[:], gl[:], over(gm[:], [P, TT, 2], 2), ALU.subtract).then_inc(s["gin"], 1)
                dve.wait_ge(s["gexp"], 1)
                link(v.tensor_reduce(gs[:], gl[:], AX, ALU.add))
                link(v.reciprocal(gr[:], gs[:]))
                link(v.tensor_tensor(gl[:], gl[:], over(gr[:], [P, TT, 2], 2), ALU.mult))
                v.tensor_tensor(comb[:], oh1[:], gl[:, :, 0:1].to_broadcast([P, TT, EXP]), ALU.mult)
                link(v.tensor_tensor(tmp[:], oh2[:], gl[:, :, 1:2].to_broadcast([P, TT, EXP]), ALU.mult))
                link(v.tensor_tensor(comb[:], comb[:], tmp[:], ALU.add))
                for e in range(EXP):
                    accumulate(b, s, e, x1, 2 + e % 4)
                dve.wait_ge(s["acc"], EXP)

            def diagonal_attention(b):
                s = D_
                for i, dst in enumerate((qd, kd)):
                    dve.wait_ge(s["qkv"], i + 1)
                    v.tensor_scalar(dst, ps[:, i, :], bD[:, i:i + 1], P ** -0.5, ALU.add, ALU.mult).then_inc(s["qk32"], 1)
                for i, src in enumerate((qd, kd)):
                    dve.wait_ge(s["hi"], i + 1)
                    v.tensor_tensor(qk_hl[2 * i + 1].bitcast(F32R), src, qk_hl[2 * i], ALU.subtract).then_inc(s["lo"], 1)
                dve.wait_ge(s["qkv"], 3)
                v.tensor_scalar(vT, ps[:, 2, :], bD[:, 2:3], None, ALU.add).then_inc(s["v"], 1)
                for e in range(HEADS + 2):
                    if e < HEADS:
                        for half in range(2):
                            c, bank = 4 * e + 2 * half, 4 * (e % 2) + 2 * half
                            dve.wait_ge(s["score"], 2 * e + half + 1)
                            v.tensor_reduce(negm[:, c:c + 2], ps[:, bank:bank + 2, :], AX, ALU.max, negate=True
                                            ).then_inc(s["negmax"], 1)
                    d = e - 2
                    if d >= 0:
                        dve.wait_ge(s["fold"], d + 1)
                        v.tensor_reduce(diag[:, 4 * d:4 * d + 4], dg[d % 2][:, :, 0:P // 2], AX, ALU.add).then_inc(s["dsum"], 1)
                        if d % 4 == 3:
                            c = slice(4 * d - 12, 4 * d + 4)
                            v.reciprocal(rec[:, c], sums[:, c]).then_inc(s["rec"], 1)
                dve.wait_ge(s["rec"], 4)
                link(v.tensor_tensor(diag[:, c], diag[:, c], rec[:, c], ALU.mult))
                v.tensor_tensor(*weights_spread(TT - 1), ALU.mult).then_inc(s["r_last"], 1)
                for u, (bank, at) in enumerate(((0, slice(0, T - P)), (2, slice(T - P, T)))):
                    dve.wait_ge(s["spread"], u + 1)
                    v.tensor_tensor(ovT[:, at], ps[:, bank, at], vT[:, at], ALU.mult).then_inc(s["ov"], 1)
                dve.wait_ge(s["proj"], 1)

            def swiglu_experts(b):
                s = F_
                for j in range(2 * EXP + 2):
                    e, c = divmod(j, 2)
                    if j == 2:
                        dve.wait_ge(s["route"], 1)
                        link(v.tensor_copy(lg[:], YB[:, 0:TT * EXP].rearrange("p (t e) -> p t e", t=TT)))
                        pick(b, lg)
                        link(one_hot(comb, 0))
                    dve.wait_ge(s["silu"], j + 1)
                    if e >= 2 and c == 0:
                        dve.wait_ge(s["down"], e - 1)
                    v.tensor_tensor(ht[e % 2][:, c, :], ps[:, 2 * (j % 2) + 1, :], silu[j % 2], ALU.mult).then_inc(s["h"], 1)
                    if c == 1 and e >= 1:
                        accumulate(b, s, e - 1, x0, 4 + (e - 1) % 2)
                accumulate(b, s, EXP, x0, 4 + EXP % 2, weighted=False)
                dve.wait_ge(s["acc"], EXP + 1)

            link(v.tensor_copy(xh, xT_in))
            v.tensor_tensor(xl, xT_in, xh.bitcast(F32), ALU.subtract).then_inc(xl_ok, 1)
            small_heads_kv(b)
            attention(b, att["A"], TT)
            link(v.scalar_tensor_tensor(out=res[:], in0=x_in[:], scalar=2.0, in1=tiles(YB), op0=ALU.mult, op1=ALU.add))
            norm(b, 1, res, x0)
            x_lo(b, 1)
            small_heads(b)
            dve.wait_ge(B_["resid"], 1)
            link(v.tensor_tensor(res[:], tiles(YB), tiles(xb), ALU.add))
            norm(b, 2, res, x1)
            x_copy(b, 2)
            x_lo(b, 2, key32[:, 0:T])
            gelu_experts(b)
            norm(b, 3, res, x0)
            x_lo(b, 3)
            diagonal_attention(b)
            dve.wait_ge(D_["resid"], 1)
            link(v.tensor_tensor(res[:], tiles(ps[:, 1, :]), tiles(xd), ALU.add))
            norm(b, 4, res, x1)
            dve.wait_ge(xn_ok, normed(4))
            norm(b, 5, x1, x0)
            dve.wait_ge(xt_mm, 4)
            v.tensor_scalar(key32[:, T:KEYS], OB[:, 0:CTX], lnE[:, 0:1], lnE[:, 1:2], ALU.mult, ALU.add)
            dve.wait_ge(xt_mm, 5)
            v.tensor_scalar(key32[:, 0:T], YB, lnE[:, 2:3], lnE[:, 3:4], ALU.mult, ALU.add).then_inc(key_ok, 1)
            x_lo(b, 4, key32[:], KPAD)
            attention(b, att["E"], TT + 1)
            link(v.tensor_tensor(res[:], tiles(YB), x1[:], ALU.add))
            norm(b, 6, res, x0)
            x_copy(b, 6)
            swiglu_experts(b)
            norm(b, 7, res, x1)

        body.close()
        numbers = [s.num for s in signals]
        assert numbers == list(range(numbers[0], numbers[0] + len(numbers)))
        nc.sync.sem_clear(range(numbers[0], numbers[-1] + 1))
        nc.all_engine_barrier()
        loop.close()
        nc.sync.dma_start(a["out"][0], x1[:]).then_inc(last_stored, 16)
        nc.sync.wait_ge(last_stored, 16)


def kernel(**inputs):
    import numpy as np
    import concourse.bacc as bacc
    from concourse.bass_utils import run_bass_kernel_spmd

    x = {k: np.ascontiguousarray(v) for k, v in inputs.items()}
    f32 = np.float32
    cat = np.concatenate

    def by_head(w):
        return w.transpose(2, 1, 0)

    def out_proj(w):
        return w.reshape(NC, P, P).transpose(1, 0, 2)

    wkv = x["L1_xattn_Wkv"]
    part, col = np.arange(P), np.arange(P)
    after = [1, 2, 3, 0]
    spread = np.zeros((P, 4, P), f32)
    for i in range(4):
        spread[:, i, :] = col[None, :] // DB == 4 * i + part[:, None] // TH
    arrays = {
        "xT": x["x"].transpose(0, 2, 1)[after], "x": x["x"].reshape(BATCH, TT, P, P).transpose(0, 2, 1, 3)[after],
        "ctx": x["ctx_1024"][after], "cT": x["ctx_1024"].transpose(0, 2, 1)[after],
        "ident": np.eye(P, dtype=f32), "spread": spread,
        "tok_eye": (part[:, None] % TH == np.arange(TH)[None, :]).astype(f32),
        "head_mask": (part[:, None] // DB == np.arange(HEADS)[None, :]).astype(f32),
        "expert_no": np.tile(np.arange(EXP, dtype=f32), (P, 1)),
        "wqA": by_head(x["L0_attn_w_q"].transpose(1, 0, 2)), "wkA": by_head(x["L0_attn_w_k"].transpose(1, 0, 2)),
        "wqE": by_head(x["L1_xattn_Wq"].reshape(P, HEADS, DH)), "wkE": by_head(wkv[:, :INNER].reshape(P, HEADS, DH)),
        "wvA": x["L0_attn_w_v"].transpose(1, 0, 2).reshape(P, INNER), "wvE": wkv[:, INNER:],
        "woA": out_proj(x["L0_attn_w_o"]), "woE": out_proj(x["L1_xattn_Wo"]),
        "wqB": x["L0_xattn_wq"], "wkB": x["L0_xattn_wk"], "wvB": x["L0_xattn_wv"], "woB": x["L0_xattn_wo"].reshape(4, 4, DB, P).transpose(1, 0, 2, 3).reshape(P, P),
       
        "bqB": x["L0_xattn_bq"].reshape(P, 1), "bkB": x["L0_xattn_bk"].reshape(P, 1),
        "bvB": x["L0_xattn_bv"], "boB": x["L0_xattn_bo"], "boD": x["L1_attn_b_o"], "biasC": x["L0_ffn_auxfree_bias"],
        "w1C": x["L0_ffn_w1"].transpose(2, 0, 1).reshape(P, EXP * P), "w2C": x["L0_ffn_w2"].transpose(2, 0, 1),
        "rC": x["L0_ffn_router_w"].T, "rF": x["L1_ffn_router"].T,
        "wD": cat([x["L1_attn_W_q"], x["L1_attn_W_k"], x["L1_attn_W_v"]], axis=1), "woD": x["L1_attn_W_o"],
        "bD": np.stack([x["L1_attn_b_q"], x["L1_attn_b_k"], x["L1_attn_b_v"]], axis=1),
        "lnE": np.stack([x["L1_xattn_ln1_w"], x["L1_xattn_ln1_b"], x["L1_xattn_ln2_w"], x["L1_xattn_ln2_b"]], axis=1),
        "gateF": cat([x["L1_ffn_gate"], x["L1_ffn_w_gate_s"][None]]).transpose(2, 0, 1),
        "upF": cat([x["L1_ffn_up"], x["L1_ffn_w_up_s"][None]]).transpose(2, 0, 1),
        "downF": cat([x["L1_ffn_down"], x["L1_ffn_w_down_s"][None]]).transpose(2, 0, 1).reshape(2, P, EXP + 1, P)
                 .transpose(1, 2, 0, 3),
    }
    arrays = {k: np.ascontiguousarray(v) for k, v in arrays.items()}
    nc = bacc.Bacc("TRN2", target_bir_lowering=False, num_devices=1)
    aps = {k: nc.dram_tensor(k + "_dram", v.shape, mybir.dt.from_np(v.dtype), kind="ExternalInput").ap()
           for k, v in arrays.items()}
    aps["out"] = nc.dram_tensor("out_dram", (BATCH, P, TT, P), F32, kind="ExternalOutput").ap()
    build(nc, aps)
    r = run_bass_kernel_spmd(nc, [{k + "_dram": v for k, v in arrays.items()}], core_ids=[0])
    out = r.results[0]["out_dram"][after]
    return np.ascontiguousarray(out.transpose(0, 2, 1, 3).reshape(BATCH, T, P))
```
